# Optimizing a Trainium2 kernel written in Bass

```python
import numpy as np
import jax
import jax.numpy as jnp

def _softmax(x, axis=-1):
    return jax.nn.softmax(x, axis=axis)

def _gelu(x):
    return jax.nn.gelu(x, approximate=True)

def _silu(x):
    return jax.nn.silu(x)

def _sigmoid(x):
    return jax.nn.sigmoid(x)

def _layernorm(x, axis=-1, eps=1e-05):
    m = jnp.mean(x, axis=axis, keepdims=True)
    v = jnp.var(x, axis=axis, keepdims=True)
    return (x - m) / jnp.sqrt(v + eps)

def _scatter_add(tgt, idx, src, axis=0):
    return tgt.at[idx].add(src)

def _segment_sum(src, seg, n):
    return jax.ops.segment_sum(src, seg, n)
kernel_name = 'mk_xattn_ffn_d1_seqx_r4_8fc46e'

def setup_inputs(seed: int=0):
    np.random.seed(seed)
    _w = jnp.asarray

    def _rec_inputs():
        import jax
        import jax.numpy as jnp
        _rk = jax.random.key(seed)
        x = 7.22e-05 + 1 * jax.random.normal(jax.random.fold_in(_rk, 1), (16, 256, 256), jnp.float32)
        _lenS = 256 - jax.random.randint(jax.random.fold_in(_rk, 7), (16,), 0, max(1, 256 // 4) + 1, jnp.int32)
        _lenS2 = 256 - jax.random.randint(jax.random.fold_in(_rk, 8), (16,), 0, max(1, 256 // 4) + 1, jnp.int32)
        _ctx_1024P = jax.random.normal(jax.random.fold_in(_rk, 11), (16, 16, 256), jnp.float32)
        _ctx_1024c = jax.random.dirichlet(jax.random.fold_in(_rk, 511), 0.3 * jnp.ones((16,), jnp.float32), (16, 256))
        _ctx_1024t = jnp.einsum('bsk,bkd->bsd', _ctx_1024c, _ctx_1024P)
        _ctx_1024t = _ctx_1024t * jax.lax.rsqrt(jnp.mean(jnp.square(_ctx_1024t)) + 1e-12) * 0.953939
        ctx_1024 = 4.13588e-05 + 0.999923 * (_ctx_1024t + 0.3 * jax.random.normal(jax.random.fold_in(_rk, 611), (16, 256, 256), jnp.float32))
        return (x, ctx_1024)
    x, ctx_1024 = _rec_inputs()

    def _L0_xattn_setup():
        import jax, jax.numpy as jnp
        import numpy as np
        D_MODEL = 256
        NUM_HEADS = 16
        HEAD_DIM = D_MODEL // NUM_HEADS
        MAX_SEQ = 128

        def rope_tables(seq_len, dim):
            inv_freq = 1.0 / 10000.0 ** (jnp.arange(0, dim, 2, dtype=jnp.float32) / dim)
            t = jnp.arange(seq_len, dtype=jnp.float32)
            freqs = jnp.einsum('i,j->ij', t, inv_freq)
            emb = jnp.concatenate([freqs, freqs], axis=-1)
            return (jnp.cos(emb), jnp.sin(emb))

        def rotate_half(x):
            x1, x2 = jnp.split(x, 2, axis=-1)
            return jnp.concatenate([-x2, x1], axis=-1)
        key = jax.random.key(seed)
        ks = jax.random.split(key, 12)
        B, S, D = (16, 128, D_MODEL)
        s = 1.0 / np.sqrt(D)
        inp = {'query': jax.random.normal(ks[0], (B, S, D), jnp.float32), 'key': jax.random.normal(ks[1], (B, S, D), jnp.float32), 'value': jax.random.normal(ks[2], (B, S, D), jnp.float32), 'Wq': jax.random.normal(ks[3], (D, D), jnp.float32) * s, 'bq': jnp.zeros((D,), jnp.float32), 'Wk': jax.random.normal(ks[4], (D, D), jnp.float32) * s, 'bk': jnp.zeros((D,), jnp.float32), 'Wv': jax.random.normal(ks[5], (D, D), jnp.float32) * s, 'bv': jnp.zeros((D,), jnp.float32), 'Wo': jax.random.normal(ks[6], (D, D), jnp.float32) * s, 'bo': jnp.zeros((D,), jnp.float32)}
        return inp
    _L0_xattn_all = _L0_xattn_setup()
    _L0_xattn_in = {k: v for k, v in _L0_xattn_all.items() if k in ('Wq', 'bq', 'Wk', 'bk', 'Wv', 'bv', 'Wo', 'bo')}
    del _L0_xattn_all

    def _L0_ffn_setup():
        import jax, jax.numpy as jnp
        import numpy as np
        B, S, D, E = (2, 512, 256, 8)
        key = jax.random.key(seed)
        ks = jax.random.split(key, 5)
        x = jax.random.normal(ks[0], (B, S, D), dtype=jnp.float32)
        router_w = jax.random.normal(ks[1], (E, D), dtype=jnp.float32) * 0.02
        router_b = jnp.zeros((E,), dtype=jnp.float32)
        expert_w = jax.random.normal(ks[2], (E, D, D), dtype=jnp.float32) * 0.02
        expert_b = jnp.zeros((E, D), dtype=jnp.float32)
        return {'x': x, 'router_w': router_w, 'router_b': router_b, 'expert_w': expert_w, 'expert_b': expert_b}
    _L0_ffn_all = _L0_ffn_setup()
    _L0_ffn_in = {k: v for k, v in _L0_ffn_all.items() if k in ('router_w', 'router_b', 'expert_w', 'expert_b')}
    del _L0_ffn_all
    return {'x': x, 'ctx_1024': ctx_1024, 'L0_xattn_Wq': _L0_xattn_in['Wq'], 'L0_xattn_bq': _L0_xattn_in['bq'], 'L0_xattn_Wk': _L0_xattn_in['Wk'], 'L0_xattn_bk': _L0_xattn_in['bk'], 'L0_xattn_Wv': _L0_xattn_in['Wv'], 'L0_xattn_bv': _L0_xattn_in['bv'], 'L0_xattn_Wo': _L0_xattn_in['Wo'], 'L0_xattn_bo': _L0_xattn_in['bo'], 'L0_ffn_router_w': _L0_ffn_in['router_w'], 'L0_ffn_router_b': _L0_ffn_in['router_b'], 'L0_ffn_expert_w': _L0_ffn_in['expert_w'], 'L0_ffn_expert_b': _L0_ffn_in['expert_b']}

def reference(x, ctx_1024, L0_xattn_Wq, L0_xattn_bq, L0_xattn_Wk, L0_xattn_bk, L0_xattn_Wv, L0_xattn_bv, L0_xattn_Wo, L0_xattn_bo, L0_ffn_router_w, L0_ffn_router_b, L0_ffn_expert_w, L0_ffn_expert_b):
    import jax
    import jax.numpy as jnp

    def _L0_xattn_ref(query, key, value, Wq, bq, Wk, bk, Wv, bv, Wo, bo):
        import jax, jax.numpy as jnp
        import numpy as np
        D_MODEL = 256
        NUM_HEADS = 16
        HEAD_DIM = D_MODEL // NUM_HEADS
        MAX_SEQ = 128

        def rope_tables(seq_len, dim):
            inv_freq = 1.0 / 10000.0 ** (jnp.arange(0, dim, 2, dtype=jnp.float32) / dim)
            t = jnp.arange(seq_len, dtype=jnp.float32)
            freqs = jnp.einsum('i,j->ij', t, inv_freq)
            emb = jnp.concatenate([freqs, freqs], axis=-1)
            return (jnp.cos(emb), jnp.sin(emb))

        def rotate_half(x):
            x1, x2 = jnp.split(x, 2, axis=-1)
            return jnp.concatenate([-x2, x1], axis=-1)
        B, S, D = query.shape
        H, Hd = (NUM_HEADS, HEAD_DIM)
        scale = Hd ** (-0.5)

        def proj(x, W, b):
            y = jnp.einsum('bsd,ed->bse', x, W) + b
            return y.reshape(B, S, H, Hd).transpose(0, 2, 1, 3)
        q = proj(query, Wq, bq)
        k = proj(key, Wk, bk)
        v = proj(value, Wv, bv)
        cos, sin = rope_tables(S, Hd)
        cos = cos[None, None]
        sin = sin[None, None]
        q = q * cos + rotate_half(q) * sin
        k = k * cos + rotate_half(k) * sin
        attn = jnp.einsum('bhqd,bhkd->bhqk', q, k) * scale
        attn_w = jax.nn.softmax(attn, axis=-1)
        out = jnp.einsum('bhqk,bhkd->bhqd', attn_w, v)
        out = out.transpose(0, 2, 1, 3).reshape(B, S, D)
        out = jnp.einsum('bsd,ed->bse', out, Wo) + bo
        return out

    def _L0_ffn_ref(x, router_w, router_b, expert_w, expert_b):
        import jax, jax.numpy as jnp
        import numpy as np
        B, S, D, E = (2, 512, 256, 8)
        logits = jnp.einsum('bsd,ed->bse', x, router_w) + router_b
        probs = jax.nn.softmax(logits, axis=-1)
        weights = jnp.max(probs, axis=-1)
        top1 = jnp.argmax(probs, axis=-1)
        y_all = jnp.einsum('bsd,eod->bseo', x, expert_w) + expert_b
        y = jnp.take_along_axis(y_all, top1[:, :, None, None], axis=2)[:, :, 0, :]
        out = y * weights[:, :, None]
        return out
    x = x + _L0_xattn_ref(_layernorm(x, axis=-1), ctx_1024, ctx_1024, L0_xattn_Wq, L0_xattn_bq, L0_xattn_Wk, L0_xattn_bk, L0_xattn_Wv, L0_xattn_bv, L0_xattn_Wo, L0_xattn_bo)
    x = x + _L0_ffn_ref(_layernorm(x, axis=-1), L0_ffn_router_w, L0_ffn_router_b, L0_ffn_expert_w, L0_ffn_expert_b)
    return x

_drawn_inputs = setup_inputs


def setup_inputs(seed=0):
    import zlib

    import numpy as np

    out = dict(_drawn_inputs(seed))
    spreads = {'L0_xattn_bq': (0.0, 0.436),
     'L0_xattn_bk': (0.0, 0.8),
     'L0_xattn_bv': (0.0, 0.1),
     'L0_xattn_bo': (0.0, 0.1),
     'L0_ffn_router_b': (0.0, 0.286),
     'L0_ffn_expert_b': (0.0, 0.448)}
    factors = {}
    for name, (base, spread) in spreads.items():
        noise = np.random.default_rng([zlib.crc32(name.encode()), seed]).standard_normal(out[name].shape)
        drawn = base * np.exp(spread * noise) if base else spread * noise
        out[name] = jnp.asarray(drawn.astype(out[name].dtype))
    for name, factor in factors.items():
        out[name] = (out[name] * factor).astype(out[name].dtype)
    return out
```

```python
import concourse.bass as bass
from concourse import mybir
from contextlib import ExitStack
import numpy as np

F32 = mybir.dt.float32
BF16 = mybir.dt.bfloat16
I32 = mybir.dt.int32
ALU = mybir.AluOpType
ACT = mybir.ActivationFunctionType
AX = mybir.AxisListType

P = 128
D = 256
S = 256
H = 16
HD = D // H
DT = D // P
TT = S // P
HT = H // DT
NSLOT = 6
Q_PART = (0, 0, 0, 1, 1, 2)
K_PART = (0, 1, 2, 0, 1, 0)
MROW = NSLOT * HD
STACK = MROW + 3
VW = 32
SCALE = HD ** -0.5
EPS = 1e-5
E = 8
NBANK = 3
RING = 8
R_LESS, R_CHOSEN = 5, 8

SMALL = (("t0", 2), ("q0", 3), ("q1", 3), ("m1", 0), ("n0", -1), ("n1", -1), ("k", 3),
         ("a", -1), ("t1", 2), ("o0", -1), ("m0", 1), ("o1", -1), ("v", 1))
ORDER = [name for name, _ in SMALL]
BANK = dict(zip(ORDER, (0, 1, 2, 0, 1, 2, 0, 1, 2, 0, 2, 1, 2)))
READ_BY = {"q0": ("q_moved", 2, 1), "q1": ("q_moved", 2, 2), "k": ("k_moved", 1, 1), "v": ("v_moved", 1, 1),
           "t0": ("rest_made", 2, 1), "t1": ("rest_made", 2, 2), "m0": ("max_moved", 2, 1),
           "m1": ("max_moved", 2, 2), "n0": ("heads_normed", 2, 1), "n1": ("heads_normed", 2, 2),
           "a": ("normed_moved", 1, 1), "o0": ("attn_added", 2, 1), "o1": ("attn_added", 2, 2)}


class Batch:

    def __init__(self, i, c):
        self.i, self.c = i, c

    def __add__(self, n):
        return Batch(self.i, self.c + n)

    def times(self, a, b=0):
        k = a * self.c + b
        return k if isinstance(self.i, int) and self.i == 0 else self.i * (2 * a) + k

    @property
    def par(self):
        return self.c % 2

    def half(self, a, b=0):
        k = a * (self.c // 2) + b
        return k if isinstance(self.i, int) and self.i == 0 else self.i * a + k

    def after(self, n):
        return not isinstance(self.i, int) or self.c >= n

    def is_(self, n):
        return isinstance(self.i, int) and self.c == n

    def real(self, nb):
        return not isinstance(self.i, int) or 0 <= self.c < nb


def attention_moe(nc, x, x_t, ctx_t, wq, wk, wv, wo, wo_n, bq, bk, bv, bo, rope, router_t, router_b, expert_t, expert_b,
                  route, out, NB):
    NT = NB * TT
    NS = NT + E - 1
    DR = D + E
    USETS = 3
    NX = 4
    assert NS % USETS == 0 and NT % NX == 0
    R_DESC, R_TILE, R_SLOT, R_RUN, R_TRI = np.cumsum([0, E, NT, NS, E * NT]).tolist()

    with ExitStack() as ctx:
        def sb(name, shape, dt=F32):
            return ctx.enter_context(nc.sbuf_tensor(name, shape, dt))

        def pb(name):
            return ctx.enter_context(nc.psum_tensor(name, [P, 512], F32))

        def sem(name):
            return ctx.enter_context(nc.semaphore(name))

        resid = sb("resid", [P, NB * TT, D])
        w_q, w_o = (sb(n, [P, DT, DR]) for n in ("w_q", "w_o"))
        w_k, w_v = (sb(n, [P, DT, D]) for n in ("w_k", "w_v"))
        b_q, b_k, b_v, b_o = (sb(n, [P, D]) for n in ("b_q", "b_k", "b_v", "b_o"))
        cos_sin = sb("cos_sin", [P, 2, TT, D])
        avg = sb("avg", [P, P])
        ident = sb("ident", [P, P])
        ident_b = sb("ident_b", [P, P], BF16)
        powers = sb("powers", [P, TT])
        xt = [sb(f"xt{p}", [P, DT, S]) for p in range(2)]
        ct = [sb(f"ct{p}", [P, DT, S]) for p in range(2)]
        cv = [sb(f"cv{p}", [P, DT, S]) for p in range(2)]
        bn1 = sb("bn1", [P, TT, 6])
        mv1 = sb("mv1", [P, TT, 2])
        ve1 = sb("ve1", [P, 2, TT])
        rstd1 = sb("rstd1", [P, 2, TT])
        flat = sb("flat", [P, 2, TT, D])
        by_cos = sb("by_cos", [P, TT, D])
        by_sin = sb("by_sin", [P, TT, D])
        roped = [sb(f"roped{p}", [P, 2, TT, D]) for p in range(2)]
        part = [sb(f"part{t}", [P, 2, 3, S], BF16) for t in range(DT)]
        rest = sb("rest", [P, 2, S])
        stack = [sb(f"stack{p}", [P, H, 2, S], BF16) for p in range(2)]
        v_ext = [sb(f"v_ext{p}", [P, TT, H, VW]) for p in range(2)]
        nmax = sb("nmax", [P, DT, TT, HT])
        nrest = sb("nrest", [P, TT, HT])
        mpart = sb("mpart", [P, DT, TT, 3, HT], BF16)
        mrows = sb("mrows", [3 * HT, DT, S], BF16)
        prob = [sb(f"prob{n}", [P, TT, S]) for n in range(RING)]
        heads_t = sb("heads_t", [P, 4, S])
        rden = sb("rden", [P, TT, H])
        normed = sb("normed", [P, TT, D])
        normed_t = sb("normed_t", [P, DT, S])
        w_on = normed_t
        bo_col = normed
        bo_r = sb("bo_r", [P, E])
        b_r = sb("b_r", [P, E])
        table = sb("table", [P, R_TRI + P])
        w_e = sb("w_e", [P, DT, E, D])
        b_e = sb("b_e", [P, E, D])
        logit = sb("logit", [P, NT, E])
        bn2 = sb("bn2", [P, TT, 6])
        mv2 = sb("mv2", [P, TT, 2])
        mean2 = sb("mean2", [P, NT])
        ve2 = sb("ve2", [P, NT])
        rstd2 = sb("rstd2", [P, NT])
        top = sb("top", [P, NT])
        less = sb("less", [P, NT, E])
        prob_e = sb("prob_e", [P, NT, E])
        weight = sb("weight", [P, NT])
        mark = sb("mark", [P, NT, E])
        first = sb("first", [P, NT])
        chosen = sb("chosen", [P, E, NT], BF16)
        tri_b = sb("tri_b", [P, P], BF16)
        ones_b = sb("ones_b", [P, P], BF16)
        so_far = sb("so_far", [P, E, NT])
        place = sb("place", [P, E, NT])
        tiles_cmp = sb("tiles_cmp", [P, E, NS])
        tiles_of = sb("tiles_of", [P, E])
        tiles_end = sb("tiles_end", [P, E])
        slot_f = sb("slot_f", [P, NT])
        slot_i = sb("slot_i", [P, NT], I32)
        index = [sb(f"index{n}", [P, 1], I32) for n in range(NX)]
        expert_f = sb("expert_f", [P, NS])
        expert_i = sb("expert_i", [P, NS], I32)
        sorted_x = [sb(f"sorted_x{n}", [P, D]) for n in range(USETS)]
        sorted_t = [sb(f"sorted_t{n}", [P, DT, P]) for n in range(USETS)]
        sorted_y = [sb(f"sorted_y{n}", [P, D]) for n in range(USETS)]
        to_expert = [flat[:, n // TT, n % TT] for n in range(NX)]
        from_expert = [roped[0][:, n // TT, n % TT] for n in range(NX)]
        done = [roped[1][:, n // TT, n % TT] for n in range(NX)]
        zeros = sorted_y[0]

        ps_st = [pb(f"ps_st{n}") for n in range(2)]
        ps_sm = [pb(f"ps_sm{n}") for n in range(2)]
        ps_pv = pb("ps_pv")
        ps_x = [pb(f"ps_x{n}") for n in range(NBANK)]

        ps_turn = [ps_st[0], ps_st[1], ps_sm[0]]
        ps_made = [ps_sm[1], ps_pv, ps_x[2]]

        names = ["consts", "ident_made", "w_in", "x_in0", "x_in1", "q_moved", "k_moved", "v_moved", "rest_made", "max_moved", "heads_normed",
                 "normed_moved", "attn_added", "q_made", "k_made", "v_made", "turned", "max_turned", "heads_turned",
                 "normed_turned", "projected", "scores_t", "scores", "exp_done", "max_done", "pv_done",
                 "pv_moved", "stats1", "ve1_done", "rstd1_done", "bo_added", "rope_cos", "rope_sin", "rope_done",
                 "part0_made", "part1_made", "part2_made", "max_split", "rden_done", "w_mean", "w_centred", "stats2", "ve2_done",
                 "rstd2_done", "router_made", "router_ready", "routed", "exps_done", "tri_made", "counted", "e_in",
                 "slots_ready", "experts_ready", "cleared", "zero_made", "normed2", "e_turned", "e_moved", "e_made", "e_biased",
                 "picked", "index_ready", "waited"]
        s = {n: sem(n) for n in names}
        xt_in = [sem(f"xt_in{p}") for p in range(2)]
        ct_in = [sem(f"ct_in{p}") for p in range(2)]
        cv_in = [sem(f"cv_in{p}") for p in range(2)]
        stack_in = [[sem(f"stack_in{p}_{t}") for t in range(DT)] for p in range(2)]
        mrow_in = [[sem(f"mrow_in{p}_{t}") for t in range(DT)] for p in range(2)]

        scattered = [sem(f"scattered{n}") for n in range(NX)]
        sorted_in = [sem(f"sorted_in{n}") for n in range(USETS)]
        sorted_out = [sem(f"sorted_out{n}") for n in range(USETS)]
        gathered = [sem(f"gathered{n}") for n in range(NX)]
        out_done = [sem(f"out_done{n}") for n in range(NX)]
        by_expert = nc.dram_tensor("by_expert", [NS * P, D], F32).ap()
        expert_out = nc.dram_tensor("expert_out", [NS * P, D], F32).ap()

        def no_wait(eng):
            eng.sem_inc(s["waited"], 1)

        def steps(eng, step):
            first = 2
            pairs = (NB - 5 + 1 - first) // 2
            for b in range(-3, first):
                step(Batch(0, b))
            with eng.Fori(0, pairs) as i:
                step(Batch(i, first))
                step(Batch(i, first + 1))
            for b in range(first + 2 * pairs, NB + 1):
                step(Batch(0, b))

        def wait_bank_read(eng, b, name):
            n, at = ORDER.index(name), b
            while True:
                n -= 1
                if n < 0:
                    n, at = len(ORDER) - 1, at + -1
                if BANK[ORDER[n]] != BANK[name]:
                    continue
                if isinstance(at.i, int) and at.c < -3:
                    return
                of = at + SMALL[n][1]
                if of.real(NB):
                    who, per, place = READ_BY[ORDER[n]]
                    eng.wait_ge(s[who], of.times(per, place))
                    return

        x_v = x.rearrange("b (t p) d -> p (b t) d", p=P)
        NW = 13
        block = ctx.enter_context(nc.Block())

        @block.sync
        def _(sp):
            def load_t(b):
                if not b.real(NB):
                    return
                if b.after(2):
                    sp.wait_ge(s["q_made"], b.times(2, -2))
                    sp.wait_ge(s["k_made"], b.times(1, -1))
                sp.dma_start(xt[b.par][:], x_t[bass.ds(b.times(1), 1)].rearrange("b p t s -> p (b t) s")).then_inc(xt_in[b.par], 16)
                sp.dma_start(ct[b.par][:], ctx_t[bass.ds(b.times(1), 1)].rearrange("b p t s -> p (b t) s")).then_inc(ct_in[b.par], 16)

            def load_v(b):
                if not b.real(NB):
                    return
                if b.after(2):
                    sp.wait_ge(s["v_made"], b.times(1, -1))
                sp.dma_start(cv[b.par][:], ctx_t[bass.ds(b.times(1), 1)].rearrange("b p t s -> p (b t) s")).then_inc(cv_in[b.par], 16)

            def fill_stack(b, t):
                if not b.real(NB):
                    return
                sp.wait_ge(s["part2_made"], b.times(2, t + 1))
                no_wait(sp)
                if b.after(2):
                    sp.wait_ge(s["scores_t"], b.times(H, -2 * H + HT * (t + 1)))
                both = part[t][:].rearrange("p a n s -> p (a n) s")
                for slot in range(NSLOT):
                    first, second = Q_PART[slot], 3 + K_PART[slot]
                    sp.dma_start(stack[b.par][HD * slot:HD * (slot + 1), HT * t:HT * (t + 1)],
                                 both[:, first:second + 1:second - first]).then_inc(stack_in[b.par][t], 16)

            def fill_max(b, t):
                if not b.real(NB):
                    return
                sp.wait_ge(s["max_moved"], b.times(2, t + 1))
                sp.dma_start(stack[b.par][MROW:STACK, HT * t:HT * (t + 1), 0], mrows[:, t]).then_inc(mrow_in[b.par][t], 16)

            for w_sb, w in ((w_q, wq), (w_k, wk), (w_v, wv), (w_o, wo)):
                sp.dma_start(w_sb[:, :, 0:D], w.rearrange("(t p) e -> p t e", p=P)).then_inc(s["w_in"], 16)
            load_t(Batch(0, 0))
            sp.dma_start(w_q[:, :, D:], router_t.rearrange("(t p) e -> p t e", p=P)).then_inc(s["w_in"], 16)
            sp.dma_start(w_on[:], wo_n.rearrange("(t p) e -> p t e", p=P)).then_inc(s["w_in"], 16)
            sp.dma_start(bo_col[:, :, 0:1], bo.rearrange("(t p a) -> p t a", p=P, a=1),
                         allow_slow_non_contiguous=True).then_inc(s["w_in"], 16)
            for w_sb, w in ((b_q, bq), (b_k, bk), (b_v, bv), (b_o, bo), (b_r, router_b)):
                sp.dma_start(w_sb[:], w.partition_broadcast(P)).then_inc(s["w_in"], 16)
            sp.dma_start(cos_sin[:], rope).then_inc(s["w_in"], 16)

            sp.dma_start(resid[:, 0:2 * TT], x_v[:, 0:2 * TT]).then_inc(s["x_in0"], 16)
            sp.wait_ge(s["consts"], 8)

            def step(b):
                load_t(b + 4)
                load_v(b + 2)
                if b.is_(-3):
                    sp.dma_start(resid[:, 2 * TT:], x_v[:, 2 * TT:]).then_inc(s["x_in1"], 16)
                if b.is_(0):
                    for e_sb, e in ((w_e, expert_t), (b_e, expert_b.partition_broadcast(P)), (table, route)):
                        sp.dma_start(e_sb[:], e).then_inc(s["e_in"], 16)
                if b.is_(1):
                    sp.wait_ge(s["zero_made"], 1)
                    sp.dma_start(by_expert.rearrange("(j p) d -> p j d", p=P), zeros[:].unsqueeze(1).to_broadcast([P, NS, D]))\
                        .then_inc(s["cleared"], 16)
                fill_stack(b + 1, 1)
                fill_max(b, 1)
                fill_stack(b + 2, 0)
                fill_max(b + 1, 0)

            steps(sp, step)

            for n in range(NX):
                sp.wait_ge(scattered[n], 16 * (NT // NX))

            def load_sorted(i, u):
                sp.dma_start(sorted_x[u][:], by_expert[bass.ds(i * (USETS * P) + u * P, P)]).then_inc(sorted_in[u], 16)

            def store_sorted(i, u):
                sp.wait_ge(s["e_biased"], i * USETS + u + 1)
                sp.dma_start(expert_out[bass.ds(i * (USETS * P) + u * P, P)], sorted_y[u][:]).then_inc(sorted_out[u], 16)

            for u in range(USETS):
                load_sorted(0, u)
            with sp.Fori(0, NS // USETS - 1) as i:
                for u in range(USETS):
                    sp.wait_ge(s["e_turned"], i * USETS + u + 1)
                    load_sorted(i + 1, u)
                    store_sorted(i, u)
            for u in range(USETS):
                store_sorted(NS // USETS - 1, u)

            out_flat = out.rearrange("b s d -> (b s) d")
            with sp.Fori(0, NT // NX) as i:
                for n in range(NX):
                    sp.wait_ge(s["picked"], i * NX + n + 1)
                    sp.dma_start(out_flat[bass.ds(i * (NX * P) + n * P, P)], done[n]).then_inc(out_done[n], 16)
            for n in range(NX):
                sp.wait_ge(out_done[n], 16 * (NT // NX))

        @block.tensor
        def _(pe):
            mm = nc.tensor.matmul

            pe.wait_ge(s["w_in"], 16 * NW)
            pe.wait_ge(s["consts"], 8)
            pe.wait_ge(s["ident_made"], 4)
            for t in range(DT):
                last = mm(ps_pv[:, 0:DR], avg[:], w_q[:, t], start=t == 0, stop=t == DT - 1)
            last.then_inc(s["w_mean"], 1)
            pe.wait_ge(s["w_centred"], DT)
            for m in range(DT):
                for t in range(DT):
                    mm(ps_st[0][:, E * m:E * (m + 1)], w_on[:, t, P * m:P * (m + 1)], w_q[:, t, D:], start=t == 0, stop=t == DT - 1)
            pe.wait_ge(s["router_ready"], 1)
            for t in range(DT):
                last = mm(ps_st[0][:, E * DT:E * (DT + 1)], bo_col[:, t, 0:P], w_q[:, t, D:], start=t == 0, stop=t == DT - 1)
            last.then_inc(s["router_made"], 1)

            def project_q(b, n):
                if not b.real(NB):
                    return
                if n == 0:
                    pe.wait_ge(xt_in[b.par], b.half(16, 16))
                wait_bank_read(pe, b + -3, f"q{n}")
                for t in range(DT):
                    last = mm(ps_x[BANK[f"q{n}"]][:, 0:DR], xt[b.par][:, t, P * n:P * (n + 1)], w_q[:, t],
                              start=t == 0, stop=t == DT - 1)
                last.then_inc(s["q_made"], 1)

            def project_kv(b, step, name, n, src, w, arrived, made):
                if not b.real(NB):
                    return
                if n == 0:
                    pe.wait_ge(arrived[b.par], b.half(16, 16))
                    wait_bank_read(pe, step, name)
                for t in range(DT):
                    last = mm(ps_x[BANK[name]][:, D * n:D * (n + 1)], src[b.par][:, t, P * n:P * (n + 1)], w[:, t],
                              start=t == 0, stop=t == DT - 1)
                if n == TT - 1:
                    last.then_inc(s[made], 1)

            def turn(b, t):
                if not b.real(NB):
                    return
                pe.wait_ge(s["rope_done"], b.times(2, 2))
                wait_bank_read(pe, b + -2, f"t{t}")
                bank = ps_x[BANK[f"t{t}"]]
                for qk in range(2):
                    for n in range(TT):
                        last = nc.tensor.transpose(bank[:, S * qk + P * n:S * qk + P * (n + 1)],
                                                   roped[b.par][:, qk, n, P * t:P * (t + 1)], ident[:])
                last.then_inc(s["turned"], 1)

            def turn_max(b, step, t):
                if not b.real(NB):
                    return
                pe.wait_ge(s["max_split"], b.times(8, 4 * (t + 1)))
                wait_bank_read(pe, step, f"m{t}")
                bank = ps_x[BANK[f"m{t}"]][:].bitcast(BF16)
                for n in range(TT):
                    last = nc.tensor.transpose(bank[0:3 * HT, P * n:P * (n + 1)],
                                               mpart[:, t, n].rearrange("p a h -> p (a h)"), ident_b[:])
                last.then_inc(s["max_turned"], 1)

            def score_t(b, h):
                if not b.real(NB):
                    return
                if h % HT == 0:
                    pe.wait_ge(mrow_in[b.par][h // HT], b.half(16, 16))
                if h >= 2 or b.after(1):
                    pe.wait_ge(s["exp_done"], b.times(H, h - 1))
                for n in range(TT):
                    last = mm(ps_st[h % 2][:, S * n:S * (n + 1)], stack[b.par][0:STACK, h, 1, P * n:P * (n + 1)],
                              stack[b.par][0:STACK, h, 0, :], start=True, stop=True)
                last.then_inc(s["scores_t"], 1)

            def score(b, h):
                if not b.real(NB):
                    return
                if h % HT == 0:
                    pe.wait_ge(stack_in[b.par][h // HT], b.half(16 * NSLOT, 16 * NSLOT))
                if h >= 2 or b.after(1):
                    pe.wait_ge(s["max_done"], b.times(H, h - 1))
                for n in range(TT):
                    last = mm(ps_sm[h % 2][:, S * n:S * (n + 1)], stack[b.par][0:MROW, h, 0, P * n:P * (n + 1)],
                              stack[b.par][0:MROW, h, 1, :], start=True, stop=True)
                last.then_inc(s["scores"], 1)

            def prob_v(b, g):
                if not b.real(NB):
                    return
                pe.wait_ge(s["exp_done"], b.times(H, 4 * g + 4))
                if g == 0:
                    pe.wait_ge(s["v_moved"], b.times(1, 1))
                if g % 2 == 0 and (g or b.after(1)):
                    pe.wait_ge(s["pv_moved"], b.times(2, g // 2))
                for n in range(TT):
                    for j in range(4):
                        h = 4 * g + j
                        last = mm(ps_pv[32 * j:32 * (j + 1), S * (g % 2):S * (g % 2 + 1)], v_ext[b.par][:, n, h, :],
                                  prob[h % RING][:, n, :], start=n == 0, stop=n == TT - 1)
                last.then_inc(s["pv_done"], 1)

            def turn_heads(b, n):
                if not b.real(NB):
                    return
                pe.wait_ge(s["pv_moved"], b.times(2, 2))
                wait_bank_read(pe, b + 1, f"n{n}")
                for g in range(4):
                    last = nc.tensor.transpose(ps_x[BANK[f"n{n}"]][:, P * g:P * (g + 1)], heads_t[:, g, P * n:P * (n + 1)], ident[:])
                last.then_inc(s["heads_turned"], 1)

            def turn_normed(b):
                if not b.real(NB):
                    return
                pe.wait_ge(s["heads_normed"], b.times(2, 2))
                wait_bank_read(pe, b + 1, "a")
                for t in range(DT):
                    for n in range(TT):
                        last = nc.tensor.transpose(ps_x[BANK["a"]][:, S * t + P * n:S * t + P * (n + 1)],
                                                   normed[:, n, P * t:P * (t + 1)], ident[:])
                last.then_inc(s["normed_turned"], 1)

            def project_out(b, n):
                if not b.real(NB):
                    return
                if n == 0:
                    pe.wait_ge(s["normed_moved"], b.times(1, 1))
                    if b.is_(0):
                        pe.wait_ge(s["router_ready"], 3)
                wait_bank_read(pe, b + 1, f"o{n}")
                for t in range(DT):
                    last = mm(ps_x[BANK[f"o{n}"]][:, 0:DR], normed_t[:, t, P * n:P * (n + 1)], w_o[:, t],
                              start=t == 0, stop=t == DT - 1)
                last.then_inc(s["projected"], 1)

            def step(b):
                def k_of(n):
                    project_kv(b + 3, b, "k", n, ct, w_k, ct_in, "k_made")

                def v_of(n):
                    project_kv(b + 1, b, "v", n, cv, w_v, cv_in, "v_made")

                small = {
                    0: lambda: turn(b + 2, 0),
                    1: lambda: prob_v(b + -1, 3),
                    2: lambda: project_q(b + 3, 0),
                    3: lambda: (project_q(b + 3, 1), turn_max(b, b, 1)),
                    4: lambda: turn_heads(b + -1, 0),
                    5: lambda: turn_heads(b + -1, 1),
                    6: lambda: prob_v(b, 0),
                    7: lambda: k_of(0),
                    8: lambda: k_of(1),
                    9: lambda: (turn_normed(b + -1), turn(b + 2, 1)),
                    10: lambda: prob_v(b, 1),
                    11: lambda: project_out(b + -1, 0),
                    12: lambda: (turn_max(b + 1, b, 0), project_out(b + -1, 1)),
                    13: lambda: prob_v(b, 2),
                    14: lambda: v_of(0),
                    15: lambda: v_of(1),
                }
                for h in range(H):
                    score_t(b, h)
                    score(b + 1, h)
                    if h in small:
                        small[h]()

            steps(pe, step)

            pe.wait_ge(s["routed"], R_CHOSEN)
            pe.wait_ge(s["tri_made"], 2)
            flat_chosen = chosen[:].rearrange("p e n -> p (e n)")
            mm(ps_x[0][:, 0:E * NT], tri_b[:], flat_chosen, start=True, stop=True)
            mm(ps_x[1][:, 0:E * NT], ones_b[:], flat_chosen, start=True, stop=True).then_inc(s["counted"], 1)

            pe.wait_ge(s["experts_ready"], 1)
            pe.wait_ge(s["e_in"], 16 * 3)

            def expert(i, u, warm):
                pe.wait_ge(sorted_in[u], i * 16 + 16)
                if warm:
                    pe.wait_ge(s["e_moved"], i * USETS + (u + 1 - USETS))
                for t in range(DT):
                    last = nc.tensor.transpose(ps_turn[u][:, P * t:P * (t + 1)], sorted_x[u][:, P * t:P * (t + 1)], ident[:])
                last.then_inc(s["e_turned"], 1)
                e = pe.value_load(expert_i[0:1, bass.ds(i * USETS + u, 1)], min_val=0, max_val=E - 1)
                pe.wait_ge(s["e_moved"], i * USETS + u + 1)
                if warm:
                    pe.wait_ge(s["e_biased"], i * USETS + (u + 1 - USETS))
                for t in range(DT):
                    last = mm(ps_made[u][:, 0:D], sorted_t[u][:, t], w_e[:, t, bass.ds(e, 1)].rearrange("p e d -> p (e d)"),
                              start=t == 0, stop=t == DT - 1)
                last.then_inc(s["e_made"], 1)

            for u in range(USETS):
                expert(0, u, False)
            with pe.Fori(1, NS // USETS) as i:
                for u in range(USETS):
                    expert(i, u, True)

        @block.scalar
        def _(act):
            def exp(b, h):
                if not b.real(NB):
                    return
                act.wait_ge(s["scores_t"], b.times(H, h + 1))
                g = h // 4
                if g >= 2 or b.after(1):
                    act.wait_ge(s["pv_done"], b.times(4, g - 1))
                nc.scalar.activation(prob[h % RING][:].rearrange("p n s -> p (n s)"), ps_st[h % 2][:], ACT.Exp,
                                     scale=SCALE).then_inc(s["exp_done"], 1)

            def move_max(b, t):
                if not b.real(NB):
                    return
                act.wait_ge(s["max_turned"], b.times(2, t + 1))
                if b.after(1):
                    act.wait_ge(mrow_in[(b + -1).par][t], (b + -1).half(16, 16))
                nc.scalar.copy(mrows[:, t], ps_x[BANK[f"m{t}"]][:].bitcast(BF16)[0:3 * HT, 0:S]).then_inc(s["max_moved"], 1)

            def move_heads(b, half):
                if not b.real(NB):
                    return
                act.wait_ge(s["pv_done"], b.times(4, 2 * half + 2))
                if b.after(1):
                    act.wait_ge(s["heads_turned"], b.times(2))
                nc.scalar.copy(heads_t[:, 2 * half:2 * half + 2].rearrange("p g s -> p (g s)"), ps_pv[:]).then_inc(s["pv_moved"], 1)

            def part0(b, t):
                if not b.real(NB):
                    return
                act.wait_ge(s["turned"], b.times(2, t + 1))
                if b.after(1):
                    o = b + -1
                    act.wait_ge(stack_in[o.par][t], o.half(16 * NSLOT, 16 * NSLOT))
                nc.scalar.copy(part[t][:, :, 0], ps_x[BANK[f"t{t}"]][:].rearrange("p (a s) -> p a s", a=2)).then_inc(s["part0_made"], 1)

            def part1(b, t):
                if not b.real(NB):
                    return
                act.wait_ge(s["rest_made"], b.times(2, t + 1))
                nc.scalar.copy(part[t][:, :, 1], rest[:]).then_inc(s["part1_made"], 1)

            def move_normed(b):
                if not b.real(NB):
                    return
                act.wait_ge(s["normed_turned"], b.times(1, 1))
                if b.after(1):
                    act.wait_ge(s["projected"], b.times(2))
                nc.scalar.copy(normed_t[:].rearrange("p t s -> p (t s)"), ps_x[BANK["a"]][:]).then_inc(s["normed_moved"], 1)

            def step(b):
                other = {
                    0: lambda: part0(b + 2, 0),
                    2: lambda: move_heads(b + -1, 1),
                    3: lambda: part1(b + 2, 0),
                    4: lambda: move_max(b, 1),
                    9: lambda: move_normed(b + -1),
                    10: lambda: part0(b + 2, 1),
                    11: lambda: move_heads(b, 0),
                    12: lambda: move_max(b + 1, 0),
                    13: lambda: part1(b + 2, 1),
                }
                for h in range(H):
                    exp(b, h)
                    if h in other:
                        other[h]()

            steps(act, step)

            act.wait_ge(s["routed"], R_LESS)
            nc.scalar.activation(prob_e[:], less[:], ACT.Exp).then_inc(s["exps_done"], 1)

            def move_turned(i, u, warm):
                act.wait_ge(s["e_turned"], i * USETS + u + 1)
                if warm:
                    act.wait_ge(s["e_made"], i * USETS + (u + 1 - USETS))
                nc.scalar.copy(sorted_t[u][:].rearrange("p t s -> p (t s)"), ps_turn[u][:, 0:D]).then_inc(s["e_moved"], 1)

            for u in range(USETS):
                move_turned(0, u, False)
            with act.Fori(1, NS // USETS) as i:
                for u in range(USETS):
                    move_turned(i, u, True)

        @block.vector
        def _(dve):
            v = nc.vector
            v.memset(avg[:], 1.0 / D).then_inc(s["consts"], 1)
            v.memset(powers[:], -0.5).then_inc(s["consts"], 1)
            for p in range(2):
                v.memset(v_ext[p][:, :, :, HD:HD + 1], 1.0).then_inc(s["consts"], 1)
                v.memset(v_ext[p][:, :, :, HD + 1:], 0.0).then_inc(s["consts"], 1)
                v.memset(stack[p][MROW:P], 1.0).then_inc(s["consts"], 1)
            v.memset(zeros[:], 0.0).then_inc(s["zero_made"], 1)
            v.memset(ones_b[:], 1.0).then_inc(s["tri_made"], 1)
            dve.wait_ge(s["w_mean"], 1)
            for t in range(DT):
                v.tensor_tensor(w_q[:, t], w_q[:, t], ps_pv[:, 0:DR], ALU.subtract).then_inc(s["w_centred"], 1)
            v.tensor_copy(bo_col[:, :, 1:P], bo_col[:, :, 0:1].to_broadcast([P, DT, P - 1])).then_inc(s["router_ready"], 1)
            dve.wait_ge(s["router_made"], 1)
            v.tensor_copy(w_o[:, :, D:], ps_st[0][:, 0:E * DT].rearrange("p (t e) -> p t e", t=DT)).then_inc(s["router_ready"], 1)
            v.tensor_copy(bo_r[:], ps_st[0][:, E * DT:E * (DT + 1)]).then_inc(s["router_ready"], 1)

            def take_max(b, h):
                if not b.real(NB):
                    return
                dve.wait_ge(s["scores"], b.times(H, h + 1))
                if h % HT == 0 and b.after(1):
                    dve.wait_ge(s["max_split"], b.times(8, 4 * (h // HT + 1) - 8))
                v.tensor_reduce(nmax[:, h // HT, :, h % HT], ps_sm[h % 2][:].rearrange("p (n s) -> p n s", n=TT), AX.X,
                                ALU.max, negate=True).then_inc(s["max_done"], 1)

            def split_max(b, t, n):
                if not b.real(NB):
                    return
                if n == 0:
                    dve.wait_ge(s["max_done"], b.times(H, HT * (t + 1)))
                    if b.after(1):
                        dve.wait_ge(s["max_turned"], b.times(2, t - 1))
                    op = v.tensor_copy(mpart[:, t, :, 0], nmax[:, t])
                else:
                    dve.wait_ge(s["max_split"], b.times(8, 4 * t + n))
                    if n == 1:
                        op = v.tensor_tensor(nrest[:], nmax[:, t], mpart[:, t, :, 0], ALU.subtract)
                    elif n == 2:
                        op = v.tensor_copy(mpart[:, t, :, 1], nrest[:])
                    else:
                        op = v.tensor_tensor(mpart[:, t, :, 2], nrest[:], mpart[:, t, :, 1], ALU.subtract)
                op.then_inc(s["max_split"], 1)

            def stats1(b, n):
                if not b.real(NB):
                    return
                if n == 0 and b.is_(0):
                    dve.wait_ge(s["x_in0"], 16)
                if n == 0 and b.is_(2):
                    dve.wait_ge(s["x_in1"], 16)
                v.bn_stats(bn1[:, n], resid[:, bass.ds(b.times(TT, n), 1)].rearrange("p a d -> p (a d)")).then_inc(s["stats1"], 1)

            def variance1(b):
                if not b.real(NB):
                    return
                for n in range(TT):
                    dve.wait_ge(s["stats1"], b.times(4, n + 1))
                    no_wait(dve)
                    v.bn_aggr(mv1[:, n], bn1[:, n]).then_inc(s["stats1"], 1)

            def variance1_eps(b):
                if not b.real(NB):
                    return
                dve.wait_ge(s["stats1"], b.times(4, 4))
                if b.after(2):
                    dve.wait_ge(s["rstd1_done"], b.times(1, -1))
                v.tensor_scalar(ve1[:, b.par], mv1[:, :, 1], EPS, None, ALU.add).then_inc(s["ve1_done"], 1)

            def move_q(b, n):
                if not b.real(NB):
                    return
                dve.wait_ge(s["q_made"], b.times(2, n + 1))
                if n == 0:
                    dve.wait_ge(s["rstd1_done"], b.times(1, 1))
                    if b.after(1):
                        dve.wait_ge(s["rope_sin"], b.times(4, -2))
                v.scalar_tensor_tensor(flat[:, 0, n], ps_x[BANK[f"q{n}"]][:, 0:D], rstd1[:, b.par, n:n + 1], b_q[:],
                                       ALU.mult, ALU.add)
                v.tensor_copy(logit[:, bass.ds(b.times(TT, n), 1)].rearrange("p a e -> p (a e)"),
                              ps_x[BANK[f"q{n}"]][:, D:DR]).then_inc(s["q_moved"], 1)

            def move_k(b):
                if not b.real(NB):
                    return
                dve.wait_ge(s["k_made"], b.times(1, 1))
                if b.after(1):
                    dve.wait_ge(s["rope_sin"], b.times(4))
                v.tensor_tensor(flat[:, 1], ps_x[BANK["k"]][:].rearrange("p (n e) -> p n e", n=TT),
                                b_k[:].unsqueeze(1).to_broadcast([P, TT, D]), ALU.add).then_inc(s["k_moved"], 1)

            def move_v(b):
                if not b.real(NB):
                    return
                dve.wait_ge(s["v_made"], b.times(1, 1))
                if b.after(2):
                    dve.wait_ge(s["pv_done"], b.times(4, -4))
                v.tensor_tensor(v_ext[b.par][:, :, :, 0:HD], ps_x[BANK["v"]][:].rearrange("p (n h e) -> p n h e", n=TT, h=H),
                                b_v[:].rearrange("p (h e) -> p h e", h=H).unsqueeze(1).to_broadcast([P, TT, H, HD]),
                                ALU.add).then_inc(s["v_moved"], 1)

            def rest_of(b, t):
                if not b.real(NB):
                    return
                dve.wait_ge(s["part0_made"], b.times(2, t + 1))
                if t or b.after(1):
                    dve.wait_ge(s["part2_made"], b.times(2, t))
                v.tensor_tensor(rest[:], ps_x[BANK[f"t{t}"]][:].rearrange("p (a s) -> p a s", a=2),
                                part[t][:, :, 0], ALU.subtract).then_inc(s["rest_made"], 1)

            def invert_sums(b, n):
                if not b.real(NB):
                    return
                dve.wait_ge(s["heads_turned"], b.times(2, n + 1))
                pv = ps_x[BANK[f"n{n}"]][:].rearrange("p (h e) -> p h e", h=H)
                v.reciprocal(rden[:, n], pv[:, :, HD]).then_inc(s["rden_done"], 1)

            def norm_heads(b, n):
                if not b.real(NB):
                    return
                if n == 0 and b.after(1):
                    dve.wait_ge(s["normed_turned"], b.times(1))
                dve.wait_ge(s["rden_done"], b.times(2, n + 1))
                pv = ps_x[BANK[f"n{n}"]][:].rearrange("p (h e) -> p h e", h=H)
                v.tensor_tensor(normed[:, n].rearrange("p (h e) -> p h e", h=H), pv[:, :, 0:HD],
                                rden[:, n].unsqueeze(2).to_broadcast([P, H, HD]), ALU.mult).then_inc(s["heads_normed"], 1)

            def add_attn(b, n):
                if not b.real(NB):
                    return
                dve.wait_ge(s["projected"], b.times(2, n + 1))
                if n == 0:
                    dve.wait_ge(s["bo_added"], b.times(1, 1))
                    dve.wait_ge(s["q_moved"], b.times(2, 2))
                tile = bass.ds(b.times(TT, n), 1)
                r = resid[:, tile].rearrange("p a d -> p (a d)")
                lg = logit[:, tile].rearrange("p a e -> p (a e)")
                v.tensor_tensor(lg, ps_x[BANK[f"o{n}"]][:, D:DR], lg, ALU.add)
                v.tensor_tensor(r, ps_x[BANK[f"o{n}"]][:, 0:D], r, ALU.add).then_inc(s["attn_added"], 1)

            def stats2(b, n):
                if not b.real(NB):
                    return
                dve.wait_ge(s["attn_added"], b.times(2, n + 1))
                no_wait(dve)
                v.bn_stats(bn2[:, n], resid[:, bass.ds(b.times(TT, n), 1)].rearrange("p a d -> p (a d)")).then_inc(s["stats2"], 1)

            def variance2(b):
                if not b.real(NB):
                    return
                for n in range(TT):
                    dve.wait_ge(s["stats2"], b.times(4, n + 1))
                    no_wait(dve)
                    v.bn_aggr(mv2[:, n], bn2[:, n]).then_inc(s["stats2"], 1)

            def variance2_eps(b):
                if not b.real(NB):
                    return
                tiles = bass.ds(b.times(TT), TT)
                dve.wait_ge(s["stats2"], b.times(4, 4))
                v.tensor_copy(mean2[:, tiles], mv2[:, :, 0])
                v.tensor_scalar(ve2[:, tiles], mv2[:, :, 1], EPS, None, ALU.add).then_inc(s["ve2_done"], 1)

            def step(b):
                if b.is_(-3):
                    for n in range(TT):
                        stats1(Batch(0, 0), n)
                    variance1(Batch(0, 0))
                    variance1_eps(Batch(0, 0))
                other = {
                    0: lambda: (split_max(b, 1, 1), move_v(b)),
                    1: lambda: (split_max(b, 1, 2), stats1(b + 4, 0)),
                    2: lambda: (split_max(b, 1, 3), rest_of(b + 2, 0)),
                    3: lambda: move_q(b + 3, 0),
                    4: lambda: move_q(b + 3, 1),
                    5: lambda: (stats1(b + 4, 1), invert_sums(b + -1, 0)),
                    6: lambda: (norm_heads(b + -1, 0), invert_sums(b + -1, 1)),
                    7: lambda: (variance1(b + 4), norm_heads(b + -1, 1)),
                    8: lambda: (variance1_eps(b + 4), split_max(b + 1, 0, 0)),
                    9: lambda: (split_max(b + 1, 0, 1), move_k(b + 3), split_max(b + 1, 0, 2)),
                    10: lambda: split_max(b + 1, 0, 3),
                    11: lambda: rest_of(b + 2, 1),
                    12: lambda: add_attn(b + -1, 0),
                    13: lambda: add_attn(b + -1, 1),
                    14: lambda: (stats2(b + -1, 0), stats2(b + -1, 1)),
                    15: lambda: (variance2(b + -1), split_max(b + 1, 1, 0), variance2_eps(b + -1)),
                }
                for h in range(H):
                    take_max(b + 1, h)
                    if h in other:
                        other[h]()

            steps(dve, step)

            done_ops = [0]

            def then(op):
                done_ops[0] += 1
                op.then_inc(s["routed"], 1)
                dve.wait_ge(s["routed"], done_ops[0])

            def per_tile(a):
                return a.unsqueeze(2).to_broadcast([P, NT, E])

            def per_expert(a, n=NT):
                return a.unsqueeze(2).to_broadcast([P, E, n])

            def rows(lo, n):
                return table[:, lo:lo + n]

            def line(a):
                return a[:].rearrange("p e n -> p (e n)")

            dve.wait_ge(s["e_in"], 16 * 3)
            v.tensor_copy(tri_b[:], rows(R_TRI, P)).then_inc(s["tri_made"], 1)
            dve.wait_ge(s["rstd2_done"], NB)
            then(v.tensor_tensor(logit[:], logit[:], bo_r[:].unsqueeze(1).to_broadcast([P, NT, E]), ALU.add))
            then(v.tensor_tensor(logit[:], logit[:], per_tile(rstd2[:]), ALU.mult))
            then(v.tensor_tensor(logit[:], logit[:], b_r[:].unsqueeze(1).to_broadcast([P, NT, E]), ALU.add))
            then(v.tensor_reduce(top[:], logit[:], AX.X, ALU.max))
            then(v.tensor_tensor(less[:], logit[:], per_tile(top[:]), ALU.subtract))
            assert done_ops[0] == R_LESS
            then(v.scalar_tensor_tensor(mark[:], less[:], 0.0, rows(R_DESC, E).unsqueeze(1).to_broadcast([P, NT, E]),
                                        ALU.is_equal, ALU.mult))
            then(v.tensor_reduce(first[:], mark[:], AX.X, ALU.max))
            then(v.tensor_tensor(chosen[:].rearrange("p e n -> p n e"), mark[:], per_tile(first[:]), ALU.is_equal))
            assert done_ops[0] == R_CHOSEN
            dve.wait_ge(s["exps_done"], 1)
            then(v.tensor_reduce(first[:], prob_e[:], AX.X, ALU.add))
            then(v.reciprocal(weight[:], first[:]))
            dve.wait_ge(s["counted"], 1)
            counts = ps_x[1][:, 0:E * NT]
            then(v.tensor_tensor_scan(line(so_far), rows(R_RUN, E * NT), counts, 0.0, ALU.mult, ALU.add))
            then(v.tensor_tensor(tiles_cmp[:, :, 0:NT], per_expert(so_far[:, :, NT - 1]),
                                 rows(R_TILE, NT).unsqueeze(1).to_broadcast([P, E, NT]), ALU.is_gt))
            then(v.tensor_reduce(tiles_of[:], tiles_cmp[:, :, 0:NT], AX.X, ALU.add))
            then(v.tensor_tensor_scan(tiles_end[:], tiles_of[:], tiles_of[:], 0.0, ALU.add, ALU.bypass))
            then(v.tensor_tensor(tiles_of[:], tiles_end[:], tiles_of[:], ALU.subtract))
            then(v.tensor_tensor(line(place), line(so_far), counts, ALU.subtract))
            then(v.tensor_tensor(line(place), ps_x[0][:, 0:E * NT], line(place), ALU.add))
            then(v.scalar_tensor_tensor(place[:], per_expert(tiles_of[:]), float(P), place[:], ALU.mult, ALU.add))
            then(v.tensor_tensor(place[:], place[:], chosen[:], ALU.mult))
            then(v.tensor_reduce(slot_f[:], place[:].rearrange("p e n -> p n e"), AX.X, ALU.add))
            v.tensor_copy(slot_i[:], slot_f[:]).then_inc(s["slots_ready"], 1)
            then(v.tensor_tensor(tiles_cmp[:], per_expert(tiles_end[:], NS),
                                 rows(R_SLOT, NS).unsqueeze(1).to_broadcast([P, E, NS]), ALU.is_le))
            then(v.tensor_reduce(expert_f[:], tiles_cmp[:].rearrange("p e n -> p n e"), AX.X, ALU.add))
            v.tensor_scalar(expert_i[:], expert_f[:], float(E - 1), None, ALU.min).then_inc(s["experts_ready"], 1)

            def normalise(i, n, warm):
                tile = bass.ds(i * NX + n, 1)
                if warm:
                    dve.wait_ge(scattered[n], i * 16)
                v.tensor_scalar(to_expert[n], resid[:, tile].rearrange("p a d -> p (a d)"), mean2[:, tile], rstd2[:, tile],
                                ALU.subtract, ALU.mult).then_inc(s["normed2"], 1)

            dve.wait_ge(s["rope_done"], 2 * NB)
            for n in range(NX):
                normalise(0, n, False)
            with dve.Fori(1, NT // NX) as i:
                for n in range(NX):
                    normalise(i, n, True)

            dve.wait_ge(s["experts_ready"], 1)

            def add_bias(i, u, warm):
                e = dve.value_load(expert_i[0:1, bass.ds(i * USETS + u, 1)], min_val=0, max_val=E - 1)
                dve.wait_ge(s["e_made"], i * USETS + u + 1)
                if warm:
                    dve.wait_ge(sorted_out[u], i * 16)
                v.tensor_tensor(sorted_y[u][:], ps_made[u][:, 0:D], b_e[:, bass.ds(e, 1)].rearrange("p e d -> p (e d)"),
                                ALU.add).then_inc(s["e_biased"], 1)

            dve.wait_ge(s["cleared"], 16)
            for u in range(USETS):
                add_bias(0, u, False)
            with dve.Fori(1, NS // USETS) as i:
                for u in range(USETS):
                    add_bias(i, u, True)

            def finish(i, n, warm):
                tile = bass.ds(i * NX + n, 1)
                dve.wait_ge(gathered[n], i * 16 + 16)
                if warm:
                    dve.wait_ge(out_done[n], i * 16)
                v.scalar_tensor_tensor(done[n], from_expert[n], weight[:, tile], resid[:, tile].rearrange("p a d -> p (a d)"),
                                       ALU.mult, ALU.add).then_inc(s["picked"], 1)

            for n in range(NX):
                finish(0, n, False)
            with dve.Fori(1, NT // NX) as i:
                for n in range(NX):
                    finish(i, n, True)

        @block.gpsimd
        def _(pool):
            g = nc.gpsimd
            for m in (ident, ident_b):
                g.memset(m[:], 0.0).then_inc(s["ident_made"], 1)
            pool.wait_ge(s["ident_made"], 2)
            for m in (ident, ident_b):
                g.affine_select(out=m[:], in_=m[:], compare_op=ALU.not_equal, fill=1.0, base=0,
                                pattern=[[-1, P]], channel_multiplier=1).then_inc(s["ident_made"], 1)

            def rstd1_of(b):
                if not b.real(NB):
                    return
                pool.wait_ge(s["ve1_done"], b.times(1, 1))
                if b.after(2):
                    pool.wait_ge(s["q_moved"], b.times(2, -2))
                g.tensor_tensor(rstd1[:, b.par], ve1[:, b.par], powers[:], ALU.pow).then_inc(s["rstd1_done"], 1)

            def rstd2_of(b):
                if not b.real(NB):
                    return
                tiles = bass.ds(b.times(TT), TT)
                pool.wait_ge(s["ve2_done"], b.times(1, 1))
                g.tensor_tensor(rstd2[:, tiles], ve2[:, tiles], powers[:], ALU.pow).then_inc(s["rstd2_done"], 1)

            def add_bo(b):
                if not b.real(NB):
                    return
                r = resid[:, bass.ds(b.times(TT), TT)]
                g.tensor_tensor(r, r, b_o[:].unsqueeze(1).to_broadcast([P, TT, D]), ALU.add).then_inc(s["bo_added"], 1)

            def rotate(b, qk):
                if not b.real(NB):
                    return
                if qk == 0:
                    pool.wait_ge(s["q_moved"], b.times(2, 2))
                else:
                    pool.wait_ge(s["k_moved"], b.times(1, 1))
                k = 2 * qk
                if qk or b.after(1):
                    pool.wait_ge(s["rope_done"], b.times(2, qk))
                g.tensor_tensor(by_cos[:], flat[:, qk], cos_sin[:, 0], ALU.mult).then_inc(s["rope_cos"], 1)
                src = flat[:, qk].rearrange("p n (t a c) -> p (n t) a c", t=DT, a=2)
                sin = cos_sin[:, 1].rearrange("p n (t a c) -> p (n t) a c", t=DT, a=2)
                dst = by_sin[:].rearrange("p n (t a c) -> p (n t) a c", t=DT, a=2)
                for a in range(2):
                    g.tensor_tensor(dst[:, :, a], src[:, :, 1 - a], sin[:, :, a], ALU.mult).then_inc(s["rope_sin"], 1)
                pool.wait_ge(s["rope_cos"], b.times(2, qk + 1))
                pool.wait_ge(s["rope_sin"], b.times(4, k + 2))
                if qk == 0 and b.after(2):
                    pool.wait_ge(s["turned"], b.times(2, -2))
                g.tensor_tensor(roped[b.par][:, qk], by_cos[:], by_sin[:], ALU.add).then_inc(s["rope_done"], 1)

            def part2(b, t):
                if not b.real(NB):
                    return
                pool.wait_ge(s["part1_made"], b.times(2, t + 1))
                g.tensor_tensor(part[t][:, :, 2], rest[:], part[t][:, :, 1], ALU.subtract).then_inc(s["part2_made"], 1)

            pool.wait_ge(s["w_in"], 16 * NW)
            pool.wait_ge(s["consts"], 8)

            def step(b):
                if b.is_(-3):
                    rstd1_of(Batch(0, 0))
                    add_bo(Batch(0, 0))
                part2(b + 2, 0)
                rotate(b + 3, 0)
                rotate(b + 3, 1)
                part2(b + 2, 1)
                rstd1_of(b + 4)
                add_bo(b + 4)
                rstd2_of(b + -1)

            steps(pool, step)

            pool.wait_ge(s["slots_ready"], 1)
            pool.wait_ge(s["cleared"], 16)

            def scatter(i, n, warm):
                if warm:
                    pool.wait_ge(scattered[n], i * 16)
                g.tensor_copy(index[n][:], slot_i[:, bass.ds(i * NX + n, 1)]).then_inc(s["index_ready"], 1)
                pool.wait_ge(s["normed2"], i * NX + n + 1)
                pool.wait_ge(s["index_ready"], i * NX + n + 1)
                no_wait(pool)
                g.indirect_dma_start(out=by_expert, out_offset=bass.IndirectOffsetOnAxis(ap=index[n][:], axis=0),
                                     in_=to_expert[n], in_offset=None).then_inc(scattered[n], 16)

            for n in range(NX):
                scatter(0, n, False)
            with pool.Fori(1, NT // NX) as i:
                for n in range(NX):
                    scatter(i, n, True)
            for n in range(NX):
                pool.wait_ge(scattered[n], 16 * (NT // NX))

            for u in range(USETS):
                pool.wait_ge(sorted_out[u], 16 * (NS // USETS))

            def gather(i, n, warm):
                if warm:
                    pool.wait_ge(s["picked"], i * NX + (n + 1 - NX))
                g.tensor_copy(index[n][:], slot_i[:, bass.ds(i * NX + n, 1)]).then_inc(s["index_ready"], 1)
                pool.wait_ge(s["index_ready"], i * NX + (NT + n + 1))
                no_wait(pool)
                g.indirect_dma_start(out=from_expert[n], out_offset=None, in_=expert_out,
                                     in_offset=bass.IndirectOffsetOnAxis(ap=index[n][:], axis=0)).then_inc(gathered[n], 16)

            for n in range(NX):
                gather(0, n, False)
            with pool.Fori(1, NT // NX) as i:
                for n in range(NX):
                    gather(i, n, True)


def rope_table():
    freq = (1.0 / np.float32(10000.0) ** (np.arange(0, HD, 2, dtype=np.float32) / np.float32(HD))).astype(np.float32)
    angle = np.arange(S, dtype=np.float32)[:, None] * freq[None]
    angle = np.concatenate([angle, angle], -1)
    cos, sin = np.cos(angle), np.sin(angle)
    sin[:, :HD // 2] *= -1
    t = np.stack([cos, sin]).astype(np.float32)
    t = np.broadcast_to(t[:, :, None, :, None], (2, S, DT, HD, HT)).reshape(2, TT, P, D)
    return np.ascontiguousarray(t.transpose(2, 0, 1, 3))


def route_table(nt):
    run = np.ones((E, nt), np.float32)
    run[:, 0] = 0
    row = np.concatenate([np.arange(E, 0, -1), P * np.arange(nt), np.arange(nt + E - 1), run.ravel()])
    return np.concatenate([np.broadcast_to(row, (P, row.size)), np.triu(np.ones((P, P)), 1)], 1).astype(np.float32)


def laid_out(inputs):
    a = {k: np.asarray(v) for k, v in inputs.items()}

    def transposed(t):
        return t.transpose(0, 2, 1).reshape(-1, DT, P, S).transpose(0, 2, 1, 3)

    def by_dim(w):
        return w.reshape(-1, DT, HT, HD).transpose(0, 1, 3, 2).reshape(w.shape)

    p = "L0_xattn_"
    return {k: np.ascontiguousarray(v) for k, v in {
        "x": a["x"], "x_t": transposed(a["x"]), "ctx_t": transposed(a["ctx_1024"]),
        "wq": by_dim(a[p + "Wq"].T), "wk": by_dim(a[p + "Wk"].T), "wv": a[p + "Wv"].T, "wo": a[p + "Wo"].T,
        "bq": by_dim(a[p + "bq"][None])[0], "bk": by_dim(a[p + "bk"][None])[0], "bv": a[p + "bv"], "bo": a[p + "bo"],
        "wo_n": a[p + "Wo"], "rope": rope_table(), "router_t": a["L0_ffn_router_w"].T, "router_b": a["L0_ffn_router_b"],
        "expert_t": a["L0_ffn_expert_w"].transpose(2, 0, 1).reshape(DT, P, E, D).transpose(1, 0, 2, 3),
        "expert_b": a["L0_ffn_expert_b"], "route": route_table(a["x"].shape[0] * TT),
    }.items()}


def kernel(**inputs):
    import concourse.bacc as bacc
    from concourse.bass_utils import run_bass_kernel_spmd

    arrays = laid_out(inputs)
    nc = bacc.Bacc("TRN2", target_bir_lowering=False, num_devices=1)
    args = {k: nc.dram_tensor(f"in_{k}", v.shape, mybir.dt.from_np(v.dtype), kind="ExternalInput").ap() for k, v in arrays.items()}
    out = nc.dram_tensor("out", arrays["x"].shape, F32, kind="ExternalOutput").ap()
    attention_moe(nc, **args, out=out, NB=arrays["x"].shape[0])
    r = run_bass_kernel_spmd(nc, [{f"in_{k}": v for k, v in arrays.items()}], core_ids=[0])
    return r.results[0]["out"]
```

```python
import concourse.bass as bass
from concourse import mybir
from contextlib import ExitStack
import numpy as np

F32 = mybir.dt.float32
BF16 = mybir.dt.bfloat16
I32 = mybir.dt.int32
ALU = mybir.AluOpType
ACT = mybir.ActivationFunctionType
AX = mybir.AxisListType

P = 128
D = 256
S = 256
H = 16
HD = D // H
DT = D // P
TT = S // P
HT = H // DT
NSLOT = 6
Q_PART = (0, 0, 0, 1, 1, 2)
K_PART = (0, 1, 2, 0, 1, 0)
MROW = NSLOT * HD
STACK = MROW + 3
VW = 32
SCALE = HD ** -0.5
EPS = 1e-5
E = 8
NBANK = 3
RING = 8
ROW = D + 4
C_RSTD, C_SHIFT, C_WEIGHT, C_ID = range(D, ROW)
ROUTE_OPS = 15
R_LESS, R_CHOSEN, R_COUNTED = 5, 8, 12
PAIR_OF_ONES = float(np.array([0x3F803F80], np.uint32).view(np.float32)[0])
ROPE_VECTOR = 2
USETS = 9
TBANK = 3

SMALL = (("t0", 2), ("q0", 3), ("q1", 3), ("m1", 0), ("n0", -1), ("n1", -1), ("k", 3),
         ("a", -1), ("t1", 2), ("o0", -1), ("m0", 1), ("o1", -1), ("c", -2), ("v", 1))
ORDER = [name for name, _ in SMALL]
BANK = dict(zip(ORDER, (0, 1, 2, 0, 1, 2, 0, 1, 2, 0, 2, 1, 0, 2)))
READ_BY = {"q0": ("q_moved", 2, 1), "q1": ("q_moved", 2, 2), "k": ("k_moved", 1, 1), "v": ("v_moved", 1, 1),
           "t0": ("rest_made", 2, 1), "t1": ("rest_made", 2, 2), "m0": ("max_moved", 2, 1),
           "m1": ("max_moved", 2, 2), "n0": ("heads_normed", 2, 1), "n1": ("heads_normed", 2, 2),
           "a": ("normed_moved", 1, 1), "o0": ("attn_added", 2, 1), "o1": ("attn_added", 2, 2),
           "c": ("routed", ROUTE_OPS, R_COUNTED)}


class Batch:

    def __init__(self, i, c, per=2):
        self.i, self.c, self.per = i, c, per

    def __add__(self, n):
        return Batch(self.i, self.c + n, self.per)

    @property
    def fixed(self):
        return isinstance(self.i, int)

    def times(self, a, b=0):
        k = a * self.c + b
        assert k >= 0 and (self.fixed or not b or k > 0)
        return k if self.fixed else self.i * (self.per * a) + k

    @property
    def par(self):
        return self.c % self.per

    def half(self, a, b=0):
        k = a * (self.c // self.per) + b
        assert k >= 0 and (self.fixed or not b or k > 0)
        return k if self.fixed else self.i * a + k

    def after(self, n):
        assert self.fixed or self.c >= n
        return self.c >= n

    def is_(self, n):
        return self.fixed and self.c == n

    def real(self, n):
        return not self.fixed or 0 <= self.c < n


def attention_moe(nc, x, x_t, ctx_t, wq, wk, wv, wo, wo_n, bias, bo_by_row, rope, expert_t, expert_b,
                  route, pads, token_ids, out, NB):
    NT = NB * TT
    NS = NT + E - 1
    DR = D + E
    REGION = (NT + 1) * P
    R_DESC, R_TILE, R_SLOT, R_BASE, R_ROW, R_TRI = np.cumsum([0, E, NT, NS, E, NS]).tolist()

    with ExitStack() as ctx:
        def sb(name, shape, dt=F32):
            return ctx.enter_context(nc.sbuf_tensor(name, shape, dt))

        def pb(name):
            return ctx.enter_context(nc.psum_tensor(name, [P, 512], F32))

        def sem(name):
            return ctx.enter_context(nc.semaphore(name))

        resid = sb("resid", [P, NB * TT, D])
        w_q, w_o = (sb(n, [P, DT, DR]) for n in ("w_q", "w_o"))
        w_k, w_v = (sb(n, [P, DT, D]) for n in ("w_k", "w_v"))
        biases = sb("biases", [P, 4 * D + E])
        b_q, b_k, b_v, b_o = (biases[:, D * n:D * (n + 1)] for n in range(4))
        b_r = biases[:, 4 * D:]
        cos_sin = sb("cos_sin", [P, 2, TT, D])
        avg = sb("avg", [P, P])
        ident = sb("ident", [P, P])
        ident_b = sb("ident_b", [P, P], BF16)
        powers = sb("powers", [P, TT])
        xt = [sb(f"xt{p}", [P, DT, S]) for p in range(2)]
        ct = [sb(f"ct{p}", [P, DT, S]) for p in range(2)]
        cv = [sb(f"cv{p}", [P, DT, S]) for p in range(2)]
        bn1 = sb("bn1", [P, TT, 6])
        mv1 = sb("mv1", [P, TT, 2])
        ve1 = sb("ve1", [P, 2, TT])
        rstd1 = sb("rstd1", [P, 2, TT])
        flat = sb("flat", [P, 2, TT, D])
        by_cos = sb("by_cos", [P, TT, D])
        by_sin = sb("by_sin", [P, TT, D])
        roped = [sb(f"roped{p}", [P, 2, TT, D]) for p in range(2)]
        part = [sb(f"part{t}", [P, 2, 3, S], BF16) for t in range(DT)]
        rest = sb("rest", [P, 2, S])
        stack = [sb(f"stack{p}", [P, H, 2, S], BF16) for p in range(2)]
        v_ext = [sb(f"v_ext{p}", [P, TT, H, VW]) for p in range(2)]
        nmax = sb("nmax", [P, DT, TT, HT])
        nrest = sb("nrest", [P, TT, HT])
        mpart = sb("mpart", [P, DT, TT, 3, HT], BF16)
        mrows = sb("mrows", [3 * HT, DT, S], BF16)
        prob = [sb(f"prob{n}", [P, TT, S]) for n in range(RING)]
        heads_t = sb("heads_t", [P, 4, S])
        rden = sb("rden", [P, TT, H])
        normed = sb("normed", [P, TT, D])
        normed_t = sb("normed_t", [P, DT, S])
        w_on = normed_t
        bo_col = normed
        bo_row = sb("bo_row", [P, DT])
        bo_r = sb("bo_r", [P, E])
        table = sb("table", [P, R_TRI + P])
        w_e = sb("w_e", [P, DT, E, D])
        b_e = sb("b_e", [P, E, D])
        ids = sb("ids", [P, NT])
        logit = sb("logit", [P, NT, E])
        row = [sb(f"row{p}", [P, TT, ROW]) for p in range(2)]
        bn2 = sb("bn2", [P, TT, 6])
        mv2 = sb("mv2", [P, TT, 2])
        ve2 = sb("ve2", [P, TT])
        logits = sb("logits", [P, TT, E])
        top = sb("top", [P, TT])
        less = sb("less", [P, TT, E])
        prob_e = sb("prob_e", [P, TT, E])
        mark = sb("mark", [P, TT, E])
        first = sb("first", [P, TT])
        chosen = sb("chosen", [P, TT, E], BF16)
        tri_b = sb("tri_b", [P, P], BF16)
        ones_b = sb("ones_b", [P, P], BF16)
        base = sb("base", [P, E])
        place = sb("place", [P, TT, E])
        slot_f = sb("slot_f", [P, TT])
        slot_i = [sb(f"slot_i{p}", [P, TT], I32) for p in range(2)]
        count = sb("count", [P, E])
        tiles_cmp = sb("tiles_cmp", [P, E, NS])
        tiles_of = sb("tiles_of", [P, E])
        tiles_end = sb("tiles_end", [P, E])
        lead = sb("lead", [P, E + 1])
        hop = sb("hop", [P, E])
        expert_f = sb("expert_f", [P, NS])
        expert_i = sb("expert_i", [P, NS], I32)
        start_f = sb("start_f", [P, NS])
        start_i = sb("start_i", [P, NS], I32)
        sorted_x = [sb(f"sorted_x{n}", [P, ROW]) for n in range(USETS)]
        sorted_t = [sb(f"sorted_t{n}", [P, DT, P]) for n in range(TBANK)]
        index = [sb(f"index{n}", [P, 1], I32) for n in range(USETS)]
        spare = [b[:, n] for b in (by_cos, by_sin) for n in range(TT)]
        spare += [b[:, a, n] for b in (flat, *roped) for a in range(2) for n in range(TT)]
        sorted_n, spare = spare[:TBANK], spare[TBANK:]
        sorted_y, spare = spare[:TBANK], spare[TBANK:]
        done = spare[:USETS]

        ps_st = [pb(f"ps_st{n}") for n in range(2)]
        ps_sm = [pb(f"ps_sm{n}") for n in range(2)]
        ps_pv = pb("ps_pv")
        ps_x = [pb(f"ps_x{n}") for n in range(NBANK)]

        ps_turn = [ps_st[0], ps_st[1], ps_sm[0]]
        ps_made = [ps_sm[1], ps_pv, ps_x[2]]

        names = ["consts", "avg_made", "powers_made", "ident_made", "wq_in", "wk_in", "wv_in", "wo_in", "bias_in", "rope_in", "x_in0", "x_in1", "q_moved", "k_moved", "v_moved", "rest_made", "max_moved", "heads_normed",
                 "normed_moved", "attn_added", "q_made", "k_made", "v_made", "turned", "max_turned", "heads_turned",
                 "normed_turned", "projected", "scores_t", "scores", "exp_done", "max_done", "pv_done",
                 "pv_moved", "stats1", "ve1_done", "rstd1_done", "bo_added", "rope_cos", "rope_sin", "rope_done",
                 "part0_made", "part1_made", "part2_made", "max_split", "rden_done", "w_mean", "w_centred", "stats2", "ve2_done",
                 "rstd2_done", "router_made", "router_ready", "routed", "exps_done", "tri_made", "counted", "e_in",
                 "table_in", "planned", "padded", "e_normed", "e_turned", "e_moved", "e_made", "e_biased", "e_done", "waited"]
        s = {n: sem(n) for n in names}
        xt_in = [sem(f"xt_in{p}") for p in range(2)]
        ct_in = [sem(f"ct_in{p}") for p in range(2)]
        cv_in = [sem(f"cv_in{p}") for p in range(2)]
        stack_in = [[sem(f"stack_in{p}_{t}") for t in range(DT)] for p in range(2)]
        mrow_in = [[sem(f"mrow_in{p}_{t}") for t in range(DT)] for p in range(2)]

        scattered = [sem(f"scattered{p}") for p in range(2)]
        sorted_in = [sem(f"sorted_in{n}") for n in range(USETS)]
        out_done = [sem(f"out_done{n}") for n in range(USETS)]
        by_expert = nc.dram_tensor("by_expert", [E * REGION + (E - 1) * P, ROW], F32).ap()

        def no_wait(eng):
            eng.sem_inc(s["waited"], 1)

        def steps(eng, step):
            first = 4
            pairs = (NB - 5 + 1 - first) // 2
            for b in range(-3, first):
                step(Batch(0, b))
            with eng.Fori(0, pairs) as i:
                step(Batch(i, first))
                step(Batch(i, first + 1))
            for b in range(first + 2 * pairs, NB + 2):
                step(Batch(0, b))

        def sorted_steps(eng, step):
            first = USETS + 1
            rounds = (NS - 1 - first) // USETS
            for j in range(first):
                step(Batch(0, j, USETS))
            with eng.Fori(0, rounds) as i:
                for u in range(USETS):
                    step(Batch(i, first + u, USETS))
            for j in range(first + rounds * USETS, NS + 1):
                step(Batch(0, j, USETS))

        def wait_bank_read(eng, b, name):
            n, at = ORDER.index(name), b
            while True:
                n -= 1
                if n < 0:
                    n, at = len(ORDER) - 1, at + -1
                if BANK[ORDER[n]] != BANK[name]:
                    continue
                if isinstance(at.i, int) and at.c < -3:
                    return
                of = at + SMALL[n][1]
                if of.real(NB):
                    who, per, place = READ_BY[ORDER[n]]
                    eng.wait_ge(s[who], of.times(per, place))
                    return

        def rotate(eng, ve, b, qk):
            if not b.real(NB):
                return
            if b.is_(0) and qk == 0 or b.is_(ROPE_VECTOR) and qk == 0:
                eng.wait_ge(s["rope_in"], 16)
            if qk == 0:
                eng.wait_ge(s["q_moved"], b.times(2, 2))
            else:
                eng.wait_ge(s["k_moved"], b.times(1, 1))
            k = 2 * qk
            if qk or b.after(1):
                eng.wait_ge(s["rope_done"], b.times(2, qk))
            ve.tensor_tensor(by_cos[:], flat[:, qk], cos_sin[:, 0], ALU.mult).then_inc(s["rope_cos"], 1)
            src = flat[:, qk].rearrange("p n (t a c) -> p (n t) a c", t=DT, a=2)
            sin = cos_sin[:, 1].rearrange("p n (t a c) -> p (n t) a c", t=DT, a=2)
            dst = by_sin[:].rearrange("p n (t a c) -> p (n t) a c", t=DT, a=2)
            for a in range(2):
                ve.tensor_tensor(dst[:, :, a], src[:, :, 1 - a], sin[:, :, a], ALU.mult).then_inc(s["rope_sin"], 1)
            eng.wait_ge(s["rope_cos"], b.times(2, qk + 1))
            eng.wait_ge(s["rope_sin"], b.times(4, k + 2))
            if qk == 0 and b.after(2):
                eng.wait_ge(s["turned"], b.times(2, -2))
            ve.tensor_tensor(roped[b.par][:, qk], by_cos[:], by_sin[:], ALU.add).then_inc(s["rope_done"], 1)

        x_v = x.rearrange("b (t p) d -> p (b t) d", p=P)
        block = ctx.enter_context(nc.Block())

        @block.sync
        def _(sp):
            def load_t(b):
                if not b.real(NB):
                    return
                if b.after(2):
                    sp.wait_ge(s["q_made"], b.times(2, -2))
                    sp.wait_ge(s["k_made"], b.times(1, -1))
                sp.dma_start(xt[b.par][:], x_t[bass.ds(b.times(1), 1)].rearrange("b p t s -> p (b t) s")).then_inc(xt_in[b.par], 16)
                sp.dma_start(ct[b.par][:], ctx_t[bass.ds(b.times(1), 1)].rearrange("b p t s -> p (b t) s")).then_inc(ct_in[b.par], 16)

            def load_v(b):
                if not b.real(NB):
                    return
                if b.after(2):
                    sp.wait_ge(s["v_made"], b.times(1, -1))
                sp.dma_start(cv[b.par][:], ctx_t[bass.ds(b.times(1), 1)].rearrange("b p t s -> p (b t) s")).then_inc(cv_in[b.par], 16)

            def fill_stack(b, t):
                if not b.real(NB):
                    return
                sp.wait_ge(s["part2_made"], b.times(2, t + 1))
                no_wait(sp)
                if b.after(2):
                    sp.wait_ge(s["scores_t"], b.times(H, -2 * H + HT * (t + 1)))
                both = part[t][:].rearrange("p a n s -> p (a n) s")
                for slot in range(NSLOT):
                    first, second = Q_PART[slot], 3 + K_PART[slot]
                    sp.dma_start(stack[b.par][HD * slot:HD * (slot + 1), HT * t:HT * (t + 1)],
                                 both[:, first:second + 1:second - first]).then_inc(stack_in[b.par][t], 16)

            def fill_max(b, t):
                if not b.real(NB):
                    return
                sp.wait_ge(s["max_moved"], b.times(2, t + 1))
                sp.dma_start(stack[b.par][MROW:STACK, HT * t:HT * (t + 1), 0], mrows[:, t]).then_inc(mrow_in[b.par][t], 16)

            def by_row(w):
                return w.rearrange("(t p) e -> p t e", p=P)

            sp.dma_start(w_q[:], by_row(wq)).then_inc(s["wq_in"], 16)
            load_t(Batch(0, 0))
            sp.dma_start(w_k[:], by_row(wk)).then_inc(s["wk_in"], 16)
            sp.dma_start(resid[:, 0:2 * TT], x_v[:, 0:2 * TT]).then_inc(s["x_in0"], 16)
            sp.dma_start(biases[:], bias.partition_broadcast(P)).then_inc(s["bias_in"], 16)
            sp.dma_start(w_on[:], by_row(wo_n)).then_inc(s["wo_in"], 16)
            sp.dma_start(bo_row[:], bo_by_row).then_inc(s["wo_in"], 16)
            sp.dma_start(cos_sin[:], rope).then_inc(s["rope_in"], 16)
            load_t(Batch(0, 1))
            sp.dma_start(w_v[:], by_row(wv)).then_inc(s["wv_in"], 16)
            sp.dma_start(w_o[:, :, 0:D], by_row(wo)).then_inc(s["wo_in"], 16)
            def step(b):
                if not b.is_(-3):
                    load_t(b + 4)
                load_v(b + 2)
                if b.is_(-3):
                    sp.dma_start(resid[:, 2 * TT:], x_v[:, 2 * TT:]).then_inc(s["x_in1"], 16)
                if b.is_(-2):
                    sp.dma_start(table[:], route).then_inc(s["table_in"], 16)
                    sp.dma_start(ids[:], token_ids).then_inc(s["table_in"], 16)
                if b.is_(0):
                    for e_sb, e in ((w_e, expert_t), (b_e, expert_b.partition_broadcast(P))):
                        sp.dma_start(e_sb[:], e).then_inc(s["e_in"], 16)
                if b.is_(1):
                    sp.dma_start(by_expert[E * REGION:], pads[E * P:]).then_inc(s["padded"], 16)
                    sp.dma_start(by_expert[0:E * REGION].rearrange("(e r) c -> e r c", e=E)[:, 0:P],
                                 pads[0:E * P].rearrange("(e r) c -> e r c", e=E)).then_inc(s["padded"], 16)
                fill_stack(b + 1, 1)
                fill_max(b, 1)
                fill_stack(b + 2, 0)
                fill_max(b + 1, 0)

            steps(sp, step)

            sp.wait_ge(s["planned"], 2)
            for p in range(2):
                sp.wait_ge(scattered[p], 16 * TT * (NB // 2))
            sp.wait_ge(s["padded"], 16 * 2)

            def load_sorted(j):
                if not j.real(NS):
                    return
                start = sp.value_load(start_i[0:1, bass.ds(j.times(1), 1)], min_val=0, max_val=E * REGION + (E - 2) * P)
                if j.after(USETS):
                    sp.wait_ge(s["e_done"], j.times(1, 1 - USETS))
                    no_wait(sp)
                sp.dma_start(sorted_x[j.par][:], by_expert[bass.ds(start, P)]).then_inc(sorted_in[j.par], 16)

            sorted_steps(sp, load_sorted)
            for n in range(USETS):
                sp.wait_ge(out_done[n], 16 * len(range(n, NS, USETS)))

        @block.tensor
        def _(pe):
            mm = nc.tensor.matmul

            pe.wait_ge(s["wq_in"], 16)
            pe.wait_ge(s["avg_made"], 1)
            for t in range(DT):
                last = mm(ps_pv[:, 0:DR], avg[:], w_q[:, t], start=t == 0, stop=t == DT - 1)
            last.then_inc(s["w_mean"], 1)

            def fold_router(b):
                if not b.is_(-3):
                    return
                pe.wait_ge(s["wo_in"], 16 * 3)
                for m in range(DT):
                    for t in range(DT):
                        mm(ps_st[0][:, E * m:E * (m + 1)], w_on[:, t, P * m:P * (m + 1)], w_q[:, t, D:], start=t == 0, stop=t == DT - 1)
                pe.wait_ge(s["router_ready"], 1)
                for t in range(DT):
                    last = mm(ps_st[0][:, E * DT:E * (DT + 1)], bo_col[:, t, 0:P], w_q[:, t, D:], start=t == 0, stop=t == DT - 1)
                last.then_inc(s["router_made"], 1)

            def project_q(b, n):
                if not b.real(NB):
                    return
                if n == 0:
                    if b.is_(0):
                        pe.wait_ge(s["w_centred"], DT)
                    pe.wait_ge(xt_in[b.par], b.half(16, 16))
                wait_bank_read(pe, b + -3, f"q{n}")
                for t in range(DT):
                    last = mm(ps_x[BANK[f"q{n}"]][:, 0:DR], xt[b.par][:, t, P * n:P * (n + 1)], w_q[:, t],
                              start=t == 0, stop=t == DT - 1)
                last.then_inc(s["q_made"], 1)

            def project_kv(b, step, name, n, src, w, arrived, made):
                if not b.real(NB):
                    return
                if n == 0:
                    if b.is_(0):
                        pe.wait_ge(s["wk_in" if name == "k" else "wv_in"], 16)
                    pe.wait_ge(arrived[b.par], b.half(16, 16))
                    wait_bank_read(pe, step, name)
                for t in range(DT):
                    last = mm(ps_x[BANK[name]][:, D * n:D * (n + 1)], src[b.par][:, t, P * n:P * (n + 1)], w[:, t],
                              start=t == 0, stop=t == DT - 1)
                if n == TT - 1:
                    last.then_inc(s[made], 1)

            def turn(b, t):
                if not b.real(NB):
                    return
                if b.is_(0) and t == 0:
                    pe.wait_ge(s["ident_made"], 4)
                pe.wait_ge(s["rope_done"], b.times(2, 2))
                wait_bank_read(pe, b + -2, f"t{t}")
                bank = ps_x[BANK[f"t{t}"]]
                for qk in range(2):
                    for n in range(TT):
                        last = nc.tensor.transpose(bank[:, S * qk + P * n:S * qk + P * (n + 1)],
                                                   roped[b.par][:, qk, n, P * t:P * (t + 1)], ident[:])
                last.then_inc(s["turned"], 1)

            def turn_max(b, step, t):
                if not b.real(NB):
                    return
                pe.wait_ge(s["max_split"], b.times(8, 4 * (t + 1)))
                wait_bank_read(pe, step, f"m{t}")
                bank = ps_x[BANK[f"m{t}"]][:].bitcast(BF16)
                for n in range(TT):
                    last = nc.tensor.transpose(bank[0:3 * HT, P * n:P * (n + 1)],
                                               mpart[:, t, n].rearrange("p a h -> p (a h)"), ident_b[:])
                last.then_inc(s["max_turned"], 1)

            def score_t(b, h):
                if not b.real(NB):
                    return
                if h == 0 and b.is_(0):
                    pe.wait_ge(s["consts"], 6)
                if h % HT == 0:
                    pe.wait_ge(mrow_in[b.par][h // HT], b.half(16, 16))
                if h >= 2 or b.after(1):
                    pe.wait_ge(s["exp_done"], b.times(H, h - 1))
                for n in range(TT):
                    last = mm(ps_st[h % 2][:, S * n:S * (n + 1)], stack[b.par][0:STACK, h, 1, P * n:P * (n + 1)],
                              stack[b.par][0:STACK, h, 0, :], start=True, stop=True)
                last.then_inc(s["scores_t"], 1)

            def score(b, h):
                if not b.real(NB):
                    return
                if h % HT == 0:
                    pe.wait_ge(stack_in[b.par][h // HT], b.half(16 * NSLOT, 16 * NSLOT))
                if h >= 2 or b.after(1):
                    pe.wait_ge(s["max_done"], b.times(H, h - 1))
                for n in range(TT):
                    last = mm(ps_sm[h % 2][:, S * n:S * (n + 1)], stack[b.par][0:MROW, h, 0, P * n:P * (n + 1)],
                              stack[b.par][0:MROW, h, 1, :], start=True, stop=True)
                last.then_inc(s["scores"], 1)

            def prob_v(b, g):
                if not b.real(NB):
                    return
                pe.wait_ge(s["exp_done"], b.times(H, 4 * g + 4))
                if g == 0:
                    pe.wait_ge(s["v_moved"], b.times(1, 1))
                if g % 2 == 0 and (g or b.after(1)):
                    pe.wait_ge(s["pv_moved"], b.times(2, g // 2))
                for n in range(TT):
                    for j in range(4):
                        h = 4 * g + j
                        last = mm(ps_pv[32 * j:32 * (j + 1), S * (g % 2):S * (g % 2 + 1)], v_ext[b.par][:, n, h, :],
                                  prob[h % RING][:, n, :], start=n == 0, stop=n == TT - 1)
                last.then_inc(s["pv_done"], 1)

            def turn_heads(b, n):
                if not b.real(NB):
                    return
                pe.wait_ge(s["pv_moved"], b.times(2, 2))
                wait_bank_read(pe, b + 1, f"n{n}")
                for g in range(4):
                    last = nc.tensor.transpose(ps_x[BANK[f"n{n}"]][:, P * g:P * (g + 1)], heads_t[:, g, P * n:P * (n + 1)], ident[:])
                last.then_inc(s["heads_turned"], 1)

            def turn_normed(b):
                if not b.real(NB):
                    return
                pe.wait_ge(s["heads_normed"], b.times(2, 2))
                wait_bank_read(pe, b + 1, "a")
                for t in range(DT):
                    for n in range(TT):
                        last = nc.tensor.transpose(ps_x[BANK["a"]][:, S * t + P * n:S * t + P * (n + 1)],
                                                   normed[:, n, P * t:P * (t + 1)], ident[:])
                last.then_inc(s["normed_turned"], 1)

            def project_out(b, n):
                if not b.real(NB):
                    return
                if n == 0:
                    pe.wait_ge(s["normed_moved"], b.times(1, 1))
                    if b.is_(0):
                        pe.wait_ge(s["router_ready"], 3)
                wait_bank_read(pe, b + 1, f"o{n}")
                for t in range(DT):
                    last = mm(ps_x[BANK[f"o{n}"]][:, 0:DR], normed_t[:, t, P * n:P * (n + 1)], w_o[:, t],
                              start=t == 0, stop=t == DT - 1)
                last.then_inc(s["projected"], 1)

            def count_chosen(b):
                if not b.real(NB):
                    return
                pe.wait_ge(s["routed"], b.times(ROUTE_OPS, R_CHOSEN))
                if b.is_(0):
                    pe.wait_ge(s["tri_made"], 2)
                wait_bank_read(pe, b + 2, "c")
                bank = ps_x[BANK["c"]]
                ch = [chosen[:, n] for n in range(TT)]
                mm(bank[:, 0:E], tri_b[:], ch[0], start=True, stop=True)
                mm(bank[:, E:2 * E], tri_b[:], ch[1], start=True, stop=False)
                mm(bank[:, E:2 * E], ones_b[:], ch[0], start=False, stop=True)
                mm(bank[:, 2 * E:3 * E], ones_b[:], ch[0], start=True, stop=False)
                mm(bank[:, 2 * E:3 * E], ones_b[:], ch[1], start=False, stop=True).then_inc(s["counted"], 1)

            def step(b):
                def k_of(n):
                    project_kv(b + 3, b, "k", n, ct, w_k, ct_in, "k_made")

                def v_of(n):
                    project_kv(b + 1, b, "v", n, cv, w_v, cv_in, "v_made")

                small = {
                    0: lambda: turn(b + 2, 0),
                    1: lambda: prob_v(b + -1, 3),
                    2: lambda: project_q(b + 3, 0),
                    3: lambda: (project_q(b + 3, 1), fold_router(b), turn_max(b, b, 1)),
                    4: lambda: turn_heads(b + -1, 0),
                    5: lambda: turn_heads(b + -1, 1),
                    6: lambda: prob_v(b, 0),
                    7: lambda: k_of(0),
                    8: lambda: k_of(1),
                    9: lambda: (turn_normed(b + -1), turn(b + 2, 1)),
                    10: lambda: prob_v(b, 1),
                    11: lambda: project_out(b + -1, 0),
                    12: lambda: (turn_max(b + 1, b, 0), project_out(b + -1, 1)),
                    13: lambda: (count_chosen(b + -2), prob_v(b, 2)),
                    14: lambda: v_of(0),
                    15: lambda: v_of(1),
                }
                for h in range(H):
                    score_t(b, h)
                    score(b + 1, h)
                    if h in small:
                        small[h]()

            steps(pe, step)

            pe.wait_ge(s["planned"], 1)
            pe.wait_ge(s["e_in"], 16 * 2)

            def turn_sorted(j):
                if not j.real(NS):
                    return
                pe.wait_ge(s["e_normed"], j.times(1, 1))
                if j.after(TBANK):
                    pe.wait_ge(s["e_moved"], j.times(1, 1 - TBANK))
                n = j.par % TBANK
                for t in range(DT):
                    last = nc.tensor.transpose(ps_turn[n][:, P * t:P * (t + 1)], sorted_n[n][:, P * t:P * (t + 1)], ident[:])
                last.then_inc(s["e_turned"], 1)

            def expert(j):
                if not j.real(NS):
                    return
                e = pe.value_load(expert_i[0:1, bass.ds(j.times(1), 1)], min_val=0, max_val=E - 1)
                pe.wait_ge(s["e_moved"], j.times(1, 1))
                if j.after(TBANK):
                    pe.wait_ge(s["e_biased"], j.times(1, 1 - TBANK))
                n = j.par % TBANK
                for t in range(DT):
                    last = mm(ps_made[n][:, 0:D], sorted_t[n][:, t], w_e[:, t, bass.ds(e, 1)].rearrange("p e d -> p (e d)"),
                              start=t == 0, stop=t == DT - 1)
                last.then_inc(s["e_made"], 1)

            sorted_steps(pe, lambda j: (turn_sorted(j), expert(j + -1)))

        @block.scalar
        def _(act):
            def exp(b, h):
                if not b.real(NB):
                    return
                act.wait_ge(s["scores_t"], b.times(H, h + 1))
                g = h // 4
                if g >= 2 or b.after(1):
                    act.wait_ge(s["pv_done"], b.times(4, g - 1))
                nc.scalar.activation(prob[h % RING][:].rearrange("p n s -> p (n s)"), ps_st[h % 2][:], ACT.Exp,
                                     scale=SCALE).then_inc(s["exp_done"], 1)

            def move_max(b, t):
                if not b.real(NB):
                    return
                act.wait_ge(s["max_turned"], b.times(2, t + 1))
                if b.after(1):
                    act.wait_ge(mrow_in[(b + -1).par][t], (b + -1).half(16, 16))
                nc.scalar.copy(mrows[:, t], ps_x[BANK[f"m{t}"]][:].bitcast(BF16)[0:3 * HT, 0:S]).then_inc(s["max_moved"], 1)

            def move_heads(b, half):
                if not b.real(NB):
                    return
                act.wait_ge(s["pv_done"], b.times(4, 2 * half + 2))
                if b.after(1):
                    act.wait_ge(s["heads_turned"], b.times(2))
                nc.scalar.copy(heads_t[:, 2 * half:2 * half + 2].rearrange("p g s -> p (g s)"), ps_pv[:]).then_inc(s["pv_moved"], 1)

            def part0(b, t):
                if not b.real(NB):
                    return
                act.wait_ge(s["turned"], b.times(2, t + 1))
                if b.after(1):
                    o = b + -1
                    act.wait_ge(stack_in[o.par][t], o.half(16 * NSLOT, 16 * NSLOT))
                nc.scalar.copy(part[t][:, :, 0], ps_x[BANK[f"t{t}"]][:].rearrange("p (a s) -> p a s", a=2)).then_inc(s["part0_made"], 1)

            def part1(b, t):
                if not b.real(NB):
                    return
                act.wait_ge(s["rest_made"], b.times(2, t + 1))
                nc.scalar.copy(part[t][:, :, 1], rest[:]).then_inc(s["part1_made"], 1)

            def move_normed(b):
                if not b.real(NB):
                    return
                act.wait_ge(s["normed_turned"], b.times(1, 1))
                if b.after(1):
                    act.wait_ge(s["projected"], b.times(2))
                nc.scalar.copy(normed_t[:].rearrange("p t s -> p (t s)"), ps_x[BANK["a"]][:]).then_inc(s["normed_moved"], 1)

            def exp_logits(b):
                if not b.real(NB):
                    return
                act.wait_ge(s["routed"], b.times(ROUTE_OPS, R_LESS))
                nc.scalar.activation(prob_e[:], less[:], ACT.Exp).then_inc(s["exps_done"], 1)

            def step(b):
                other = {
                    0: lambda: part0(b + 2, 0),
                    2: lambda: move_heads(b + -1, 1),
                    3: lambda: part1(b + 2, 0),
                    4: lambda: move_max(b, 1),
                    8: lambda: exp_logits(b + -2),
                    9: lambda: move_normed(b + -1),
                    10: lambda: part0(b + 2, 1),
                    11: lambda: move_heads(b, 0),
                    12: lambda: move_max(b + 1, 0),
                    13: lambda: part1(b + 2, 1),
                }
                for h in range(H):
                    exp(b, h)
                    if h in other:
                        other[h]()

            steps(act, step)

            def normalise(j):
                if not j.real(NS):
                    return
                x_in = sorted_x[j.par]
                act.wait_ge(sorted_in[j.par], j.half(16, 16))
                if j.after(TBANK):
                    act.wait_ge(s["e_turned"], j.times(1, 1 - TBANK))
                nc.scalar.activation(sorted_n[j.par % TBANK], x_in[:, 0:D], ACT.Identity, bias=x_in[:, C_SHIFT:C_SHIFT + 1],
                                     scale=x_in[:, C_RSTD:C_RSTD + 1]).then_inc(s["e_normed"], 1)

            def move_turned(j):
                if not j.real(NS):
                    return
                act.wait_ge(s["e_turned"], j.times(1, 1))
                if j.after(TBANK):
                    act.wait_ge(s["e_made"], j.times(1, 1 - TBANK))
                n = j.par % TBANK
                nc.scalar.copy(sorted_t[n][:].rearrange("p t s -> p (t s)"), ps_turn[n][:, 0:D]).then_inc(s["e_moved"], 1)

            normalise(Batch(0, 0, USETS))
            sorted_steps(act, lambda j: (normalise(j + 1), move_turned(j)))

        @block.vector
        def _(dve):
            v = nc.vector
            v.memset(avg[:], 1.0 / D).then_inc(s["avg_made"], 1)
            v.memset(ones_b[:], 1.0).then_inc(s["tri_made"], 1)
            dve.wait_ge(s["w_mean"], 1)
            for t in range(DT):
                v.tensor_tensor(w_q[:, t], w_q[:, t], ps_pv[:, 0:DR], ALU.subtract).then_inc(s["w_centred"], 1)
            dve.wait_ge(s["wo_in"], 16 * 3)
            v.tensor_copy(bo_col[:, :, 0:P], bo_row[:].unsqueeze(2).to_broadcast([P, DT, P])).then_inc(s["router_ready"], 1)
            def move_router(b):
                if not b.is_(-3):
                    return
                dve.wait_ge(s["router_made"], 1)
                v.tensor_copy(w_o[:, :, D:], ps_st[0][:, 0:E * DT].rearrange("p (t e) -> p t e", t=DT)).then_inc(s["router_ready"], 1)
                v.tensor_copy(bo_r[:], ps_st[0][:, E * DT:E * (DT + 1)]).then_inc(s["router_ready"], 1)

            def early_rotate(b, qk):
                if b.fixed and b.c < ROPE_VECTOR:
                    rotate(dve, v, b, qk)

            def take_max(b, h):
                if not b.real(NB):
                    return
                dve.wait_ge(s["scores"], b.times(H, h + 1))
                if h % HT == 0 and b.after(1):
                    dve.wait_ge(s["max_split"], b.times(8, 4 * (h // HT + 1) - 8))
                v.tensor_reduce(nmax[:, h // HT, :, h % HT], ps_sm[h % 2][:].rearrange("p (n s) -> p n s", n=TT), AX.X,
                                ALU.max, negate=True).then_inc(s["max_done"], 1)

            def split_max(b, t, n):
                if not b.real(NB):
                    return
                if n == 0:
                    dve.wait_ge(s["max_done"], b.times(H, HT * (t + 1)))
                    if b.after(1):
                        dve.wait_ge(s["max_turned"], b.times(2, t - 1))
                    op = v.tensor_copy(mpart[:, t, :, 0], nmax[:, t])
                else:
                    dve.wait_ge(s["max_split"], b.times(8, 4 * t + n))
                    if n == 1:
                        op = v.tensor_tensor(nrest[:], nmax[:, t], mpart[:, t, :, 0], ALU.subtract)
                    elif n == 2:
                        op = v.tensor_copy(mpart[:, t, :, 1], nrest[:])
                    else:
                        op = v.tensor_tensor(mpart[:, t, :, 2], nrest[:], mpart[:, t, :, 1], ALU.subtract)
                op.then_inc(s["max_split"], 1)

            def stats1(b, n):
                if not b.real(NB):
                    return
                if n == 0 and b.is_(0):
                    dve.wait_ge(s["x_in0"], 16)
                if n == 0 and b.is_(2):
                    dve.wait_ge(s["x_in1"], 16)
                v.bn_stats(bn1[:, n], resid[:, bass.ds(b.times(TT, n), 1)].rearrange("p a d -> p (a d)")).then_inc(s["stats1"], 1)

            def variance1(b):
                if not b.real(NB):
                    return
                for n in range(TT):
                    dve.wait_ge(s["stats1"], b.times(4, n + 1))
                    no_wait(dve)
                    v.bn_aggr(mv1[:, n], bn1[:, n]).then_inc(s["stats1"], 1)

            def variance1_eps(b):
                if not b.real(NB):
                    return
                dve.wait_ge(s["stats1"], b.times(4, 4))
                if b.after(2):
                    dve.wait_ge(s["rstd1_done"], b.times(1, -1))
                v.tensor_scalar(ve1[:, b.par], mv1[:, :, 1], EPS, None, ALU.add).then_inc(s["ve1_done"], 1)

            def move_q(b, n):
                if not b.real(NB):
                    return
                dve.wait_ge(s["q_made"], b.times(2, n + 1))
                if n == 0:
                    dve.wait_ge(s["rstd1_done"], b.times(1, 1))
                    if b.is_(0):
                        dve.wait_ge(s["bias_in"], 16)
                        dve.wait_ge(s["router_ready"], 3)
                    if b.after(1):
                        dve.wait_ge(s["rope_sin"], b.times(4, -2))
                v.scalar_tensor_tensor(flat[:, 0, n], ps_x[BANK[f"q{n}"]][:, 0:D], rstd1[:, b.par, n:n + 1], b_q,
                                       ALU.mult, ALU.add)
                v.tensor_tensor(logit[:, bass.ds(b.times(TT, n), 1)].rearrange("p a e -> p (a e)"),
                                ps_x[BANK[f"q{n}"]][:, D:DR], bo_r[:], ALU.add).then_inc(s["q_moved"], 1)

            def move_k(b):
                if not b.real(NB):
                    return
                dve.wait_ge(s["k_made"], b.times(1, 1))
                if b.after(1):
                    dve.wait_ge(s["rope_sin"], b.times(4))
                v.tensor_tensor(flat[:, 1], ps_x[BANK["k"]][:].rearrange("p (n e) -> p n e", n=TT),
                                b_k.unsqueeze(1).to_broadcast([P, TT, D]), ALU.add).then_inc(s["k_moved"], 1)

            def move_v(b):
                if not b.real(NB):
                    return
                dve.wait_ge(s["v_made"], b.times(1, 1))
                if b.after(2):
                    dve.wait_ge(s["pv_done"], b.times(4, -4))
                v.tensor_tensor(v_ext[b.par][:, :, :, 0:HD], ps_x[BANK["v"]][:].rearrange("p (n h e) -> p n h e", n=TT, h=H),
                                b_v.rearrange("p (h e) -> p h e", h=H).unsqueeze(1).to_broadcast([P, TT, H, HD]),
                                ALU.add).then_inc(s["v_moved"], 1)

            def rest_of(b, t):
                if not b.real(NB):
                    return
                dve.wait_ge(s["part0_made"], b.times(2, t + 1))
                if t or b.after(1):
                    dve.wait_ge(s["part2_made"], b.times(2, t))
                v.tensor_tensor(rest[:], ps_x[BANK[f"t{t}"]][:].rearrange("p (a s) -> p a s", a=2),
                                part[t][:, :, 0], ALU.subtract).then_inc(s["rest_made"], 1)

            def invert_sums(b, n):
                if not b.real(NB):
                    return
                dve.wait_ge(s["heads_turned"], b.times(2, n + 1))
                pv = ps_x[BANK[f"n{n}"]][:].rearrange("p (h e) -> p h e", h=H)
                v.reciprocal(rden[:, n], pv[:, :, HD]).then_inc(s["rden_done"], 1)

            def norm_heads(b, n):
                if not b.real(NB):
                    return
                if n == 0 and b.after(1):
                    dve.wait_ge(s["normed_turned"], b.times(1))
                dve.wait_ge(s["rden_done"], b.times(2, n + 1))
                pv = ps_x[BANK[f"n{n}"]][:].rearrange("p (h e) -> p h e", h=H)
                v.tensor_tensor(normed[:, n].rearrange("p (h e) -> p h e", h=H), pv[:, :, 0:HD],
                                rden[:, n].unsqueeze(2).to_broadcast([P, H, HD]), ALU.mult).then_inc(s["heads_normed"], 1)

            def add_attn(b, n):
                if not b.real(NB):
                    return
                dve.wait_ge(s["projected"], b.times(2, n + 1))
                if n == 0:
                    dve.wait_ge(s["bo_added"], b.times(1, 1))
                    dve.wait_ge(s["q_moved"], b.times(2, 2))
                    if b.after(2):
                        dve.wait_ge(scattered[b.par], b.half(16 * TT))
                tile = bass.ds(b.times(TT, n), 1)
                v.tensor_tensor(logits[:, n], ps_x[BANK[f"o{n}"]][:, D:DR], logit[:, tile].rearrange("p a e -> p (a e)"), ALU.add)
                v.tensor_tensor(row[b.par][:, n, 0:D], ps_x[BANK[f"o{n}"]][:, 0:D], resid[:, tile].rearrange("p a d -> p (a d)"),
                                ALU.add).then_inc(s["attn_added"], 1)

            def stats2(b, n):
                if not b.real(NB):
                    return
                dve.wait_ge(s["attn_added"], b.times(2, n + 1))
                v.bn_stats(bn2[:, n], row[b.par][:, n, 0:D]).then_inc(s["stats2"], 1)

            def variance2(b):
                if not b.real(NB):
                    return
                for n in range(TT):
                    dve.wait_ge(s["stats2"], b.times(4, n + 1))
                    no_wait(dve)
                    v.bn_aggr(mv2[:, n], bn2[:, n]).then_inc(s["stats2"], 1)

            def variance2_eps(b):
                if not b.real(NB):
                    return
                dve.wait_ge(s["stats2"], b.times(4, 4))
                v.tensor_scalar(ve2[:], mv2[:, :, 1], EPS, None, ALU.add).then_inc(s["ve2_done"], 1)

            def per_tile(a):
                return a.unsqueeze(2).to_broadcast([P, TT, E])

            def each_tile(a):
                return a.unsqueeze(1).to_broadcast([P, TT, E])

            def route(b, n):
                if not b.real(NB):
                    return
                r = row[b.par]
                psum = ps_x[BANK["c"]]
                if n:
                    dve.wait_ge(s["routed"], b.times(ROUTE_OPS, n))
                if n == 0:
                    dve.wait_ge(s["rstd2_done"], b.times(1, 1))
                    op = v.tensor_tensor(logits[:], logits[:], per_tile(r[:, :, C_RSTD]), ALU.mult)
                elif n == 1:
                    op = v.scalar_tensor_tensor(r[:, :, C_SHIFT], mv2[:, :, 0], -1.0, r[:, :, C_RSTD], ALU.mult, ALU.mult)
                elif n == 2:
                    op = v.tensor_tensor(logits[:], logits[:], each_tile(b_r), ALU.add)
                elif n == 3:
                    op = v.tensor_reduce(top[:], logits[:], AX.X, ALU.max)
                elif n == 4:
                    op = v.tensor_tensor(less[:], logits[:], per_tile(top[:]), ALU.subtract)
                elif n == 5:
                    op = v.scalar_tensor_tensor(mark[:], less[:], 0.0, each_tile(table[:, R_DESC:R_DESC + E]),
                                                ALU.is_equal, ALU.mult)
                elif n == 6:
                    op = v.tensor_reduce(first[:], mark[:], AX.X, ALU.max)
                elif n == 7:
                    op = v.tensor_tensor(chosen[:], mark[:], per_tile(first[:]), ALU.is_equal)
                elif n == 8:
                    dve.wait_ge(s["exps_done"], b.times(1, 1))
                    op = v.tensor_reduce(top[:], prob_e[:], AX.X, ALU.add)
                elif n == 9:
                    op = v.reciprocal(r[:, :, C_WEIGHT], top[:])
                elif n == 10:
                    dve.wait_ge(s["counted"], b.times(1, 1))
                    op = v.tensor_tensor(place[:], psum[:, 0:TT * E].rearrange("p (n e) -> p n e", n=TT), each_tile(base[:]), ALU.add)
                elif n == 11:
                    op = v.tensor_tensor(base[:], psum[:, TT * E:(TT + 1) * E], base[:], ALU.add)
                elif n == 12:
                    op = v.tensor_tensor(place[:], place[:], chosen[:], ALU.mult)
                elif n == 13:
                    op = v.tensor_reduce(slot_f[:], place[:], AX.X, ALU.add)
                else:
                    op = v.tensor_copy(slot_i[b.par][:], slot_f[:])
                op.then_inc(s["routed"], 1)

            def number(b):
                if not b.real(NB):
                    return
                v.tensor_copy(row[b.par][:, :, C_ID], ids[:, bass.ds(b.times(TT), TT)])

            def step(b):
                if b.is_(-3):
                    for n in range(TT):
                        stats1(Batch(0, 0), n)
                    variance1(Batch(0, 0))
                    variance1_eps(Batch(0, 0))
                if b.is_(-2):
                    for p in range(2):
                        v.memset(stack[p][MROW:P, :, 1].bitcast(F32), PAIR_OF_ONES).then_inc(s["consts"], 1)
                if b.is_(-1):
                    dve.wait_ge(s["table_in"], 16 * 2)
                    v.tensor_copy(tri_b[:], table[:, R_TRI:R_TRI + P]).then_inc(s["tri_made"], 1)
                    v.tensor_copy(base[:], table[:, R_BASE:R_BASE + E]).then_inc(s["tri_made"], 1)
                other = {
                    0: lambda: (split_max(b, 1, 1), move_v(b)),
                    1: lambda: (split_max(b, 1, 2), stats1(b + 4, 0)),
                    2: lambda: (split_max(b, 1, 3), rest_of(b + 2, 0), route(b + -2, 0)),
                    3: lambda: (move_router(b), move_q(b + 3, 0), route(b + -2, 1), route(b + -2, 2)),
                    4: lambda: (move_q(b + 3, 1), early_rotate(b + 3, 0), route(b + -2, 3)),
                    5: lambda: (stats1(b + 4, 1), invert_sums(b + -1, 0), route(b + -2, 4)),
                    6: lambda: (norm_heads(b + -1, 0), invert_sums(b + -1, 1), route(b + -2, 5)),
                    7: lambda: (variance1(b + 4), norm_heads(b + -1, 1), route(b + -2, 6)),
                    8: lambda: (variance1_eps(b + 4), split_max(b + 1, 0, 0), route(b + -2, 7)),
                    9: lambda: (split_max(b + 1, 0, 1), move_k(b + 3), early_rotate(b + 3, 1),
                                split_max(b + 1, 0, 2)),
                    10: lambda: (split_max(b + 1, 0, 3), route(b + -2, 8)),
                    11: lambda: (rest_of(b + 2, 1), route(b + -2, 9)),
                    12: lambda: add_attn(b + -1, 0),
                    13: lambda: (add_attn(b + -1, 1), number(b + -1)),
                    14: lambda: (stats2(b + -1, 0), route(b + -2, 10), stats2(b + -1, 1), route(b + -2, 11)),
                    15: lambda: (route(b + -2, 12), variance2(b + -1), route(b + -2, 13), split_max(b + 1, 1, 0),
                                 variance2_eps(b + -1), route(b + -2, 14)),
                }
                for h in range(H):
                    take_max(b + 1, h)
                    if h in other:
                        other[h]()

            steps(dve, step)

            made = [ROUTE_OPS * NB]

            def then(op):
                made[0] += 1
                op.then_inc(s["routed"], 1)
                dve.wait_ge(s["routed"], made[0])

            def per_expert(a, n):
                return a.unsqueeze(2).to_broadcast([P, E, n])

            def each_expert(lo, n):
                return table[:, lo:lo + n].unsqueeze(1).to_broadcast([P, E, n])

            then(v.tensor_tensor(count[:], base[:], table[:, R_BASE:R_BASE + E], ALU.subtract))
            then(v.tensor_tensor(tiles_cmp[:, :, 0:NT], per_expert(count[:], NT), each_expert(R_TILE, NT), ALU.is_gt))
            then(v.tensor_reduce(tiles_of[:], tiles_cmp[:, :, 0:NT], AX.X, ALU.add))
            then(v.tensor_tensor_scan(tiles_end[:], tiles_of[:], tiles_of[:], 0.0, ALU.add, ALU.bypass))
            then(v.scalar_tensor_tensor(lead[:, 0:E], tiles_end[:], -float(P), base[:], ALU.mult, ALU.add))
            then(v.tensor_scalar(lead[:, E:E + 1], tiles_end[:, E - 1:E], -float(P), float(E * REGION), ALU.mult, ALU.add))
            then(v.tensor_tensor(hop[:], lead[:, 1:E + 1], lead[:, 0:E], ALU.subtract))
            then(v.tensor_tensor(tiles_cmp[:], per_expert(tiles_end[:], NS), each_expert(R_SLOT, NS), ALU.is_le))
            then(v.tensor_reduce(expert_f[:], tiles_cmp[:].rearrange("p e n -> p n e"), AX.X, ALU.add))
            v.tensor_scalar(expert_i[:], expert_f[:], float(E - 1), None, ALU.min).then_inc(s["planned"], 1)
            then(v.tensor_tensor(tiles_cmp[:], tiles_cmp[:], per_expert(hop[:], NS), ALU.mult))
            then(v.tensor_reduce(start_f[:], tiles_cmp[:].rearrange("p e n -> p n e"), AX.X, ALU.add))
            v.scalar_tensor_tensor(start_i[:], start_f[:], lead[:, 0:1], table[:, R_ROW:R_ROW + NS],
                                   ALU.add, ALU.add).then_inc(s["planned"], 1)
            dve.wait_ge(s["planned"], 1)

            def add_bias(j):
                if not j.real(NS):
                    return
                e = dve.value_load(expert_i[0:1, bass.ds(j.times(1), 1)], min_val=0, max_val=E - 1)
                n = j.par % TBANK
                dve.wait_ge(s["e_made"], j.times(1, 1))
                if j.after(TBANK):
                    dve.wait_ge(s["e_done"], j.times(1, 1 - TBANK))
                v.tensor_tensor(sorted_y[n], ps_made[n][:, 0:D], b_e[:, bass.ds(e, 1)].rearrange("p e d -> p (e d)"),
                                ALU.add).then_inc(s["e_biased"], 1)

            def finish(j):
                if not j.real(NS):
                    return
                x_in = sorted_x[j.par]
                dve.wait_ge(s["e_biased"], j.times(1, 1))
                if j.after(USETS):
                    dve.wait_ge(out_done[j.par], j.half(16))
                v.tensor_copy(index[j.par][:], x_in[:, C_ID:C_ID + 1])
                v.scalar_tensor_tensor(done[j.par], sorted_y[j.par % TBANK], x_in[:, C_WEIGHT:C_WEIGHT + 1], x_in[:, 0:D],
                                       ALU.mult, ALU.add).then_inc(s["e_done"], 1)

            sorted_steps(dve, lambda j: (add_bias(j), finish(j + -1)))

        @block.gpsimd
        def _(pool):
            g = nc.gpsimd
            g.memset(powers[:], -0.5).then_inc(s["powers_made"], 1)
            for m in (ident, ident_b):
                g.memset(m[:], 0.0).then_inc(s["ident_made"], 1)
            pool.wait_ge(s["ident_made"], 2)
            for m in (ident, ident_b):
                g.affine_select(out=m[:], in_=m[:], compare_op=ALU.not_equal, fill=1.0, base=0,
                                pattern=[[-1, P]], channel_multiplier=1).then_inc(s["ident_made"], 1)
            for p in range(2):
                g.memset(v_ext[p][:, :, :, HD:HD + 1], 1.0).then_inc(s["consts"], 1)
                g.memset(v_ext[p][:, :, :, HD + 1:], 0.0).then_inc(s["consts"], 1)

            def rstd1_of(b):
                if not b.real(NB):
                    return
                pool.wait_ge(s["ve1_done"], b.times(1, 1))
                if b.after(2):
                    pool.wait_ge(s["q_moved"], b.times(2, -2))
                g.tensor_tensor(rstd1[:, b.par], ve1[:, b.par], powers[:], ALU.pow).then_inc(s["rstd1_done"], 1)

            def rstd2_of(b):
                if not b.real(NB):
                    return
                pool.wait_ge(s["ve2_done"], b.times(1, 1))
                g.tensor_tensor(row[b.par][:, :, C_RSTD], ve2[:], powers[:], ALU.pow).then_inc(s["rstd2_done"], 1)

            def scatter(b):
                if not b.real(NB):
                    return
                pool.wait_ge(s["routed"], b.times(ROUTE_OPS, ROUTE_OPS))
                no_wait(pool)
                for n in range(TT):
                    g.indirect_dma_start(out=by_expert, out_offset=bass.IndirectOffsetOnAxis(ap=slot_i[b.par][:, n:n + 1], axis=0),
                                         in_=row[b.par][:, n], in_offset=None).then_inc(scattered[b.par], 16)

            def add_bo(b):
                if not b.real(NB):
                    return
                if b.is_(0):
                    pool.wait_ge(s["bias_in"], 16)
                r = resid[:, bass.ds(b.times(TT), TT)]
                g.tensor_tensor(r, r, b_o.unsqueeze(1).to_broadcast([P, TT, D]), ALU.add).then_inc(s["bo_added"], 1)

            def part2(b, t):
                if not b.real(NB):
                    return
                pool.wait_ge(s["part1_made"], b.times(2, t + 1))
                g.tensor_tensor(part[t][:, :, 2], rest[:], part[t][:, :, 1], ALU.subtract).then_inc(s["part2_made"], 1)

            pool.wait_ge(s["powers_made"], 1)

            def step(b):
                if b.is_(-3):
                    rstd1_of(Batch(0, 0))
                    add_bo(Batch(0, 0))
                part2(b + 2, 0)
                if b.after(ROPE_VECTOR - 3):
                    rotate(pool, g, b + 3, 0)
                    rotate(pool, g, b + 3, 1)
                part2(b + 2, 1)
                rstd1_of(b + 4)
                add_bo(b + 4)
                scatter(b + -2)
                rstd2_of(b + -1)

            steps(pool, step)

            def store_sorted(j):
                if not j.real(NS):
                    return
                pool.wait_ge(s["e_done"], j.times(1, 1))
                no_wait(pool)
                g.indirect_dma_start(out=out, out_offset=bass.IndirectOffsetOnAxis(ap=index[j.par][:], axis=0),
                                     in_=done[j.par], in_offset=None).then_inc(out_done[j.par], 16)

            sorted_steps(pool, store_sorted)


def rope_table():
    freq = (1.0 / np.float32(10000.0) ** (np.arange(0, HD, 2, dtype=np.float32) / np.float32(HD))).astype(np.float32)
    angle = np.arange(S, dtype=np.float32)[:, None] * freq[None]
    angle = np.concatenate([angle, angle], -1)
    cos, sin = np.cos(angle), np.sin(angle)
    sin[:, :HD // 2] *= -1
    t = np.stack([cos, sin]).astype(np.float32)
    t = np.broadcast_to(t[:, :, None, :, None], (2, S, DT, HD, HT)).reshape(2, TT, P, D)
    return np.ascontiguousarray(t.transpose(2, 0, 1, 3))


def route_table(nt):
    ns = nt + E - 1
    row = np.concatenate([np.arange(E, 0, -1), P * np.arange(nt), np.arange(ns), (nt + 1) * P * np.arange(E) + P, P * np.arange(ns)])
    return np.concatenate([np.broadcast_to(row, (P, row.size)), np.triu(np.ones((P, P)), 1)], 1).astype(np.float32)


def out_rows(nt):
    return (nt + 2 * E - 1) * P


def pad_rows(nt):
    pads = np.zeros((out_rows(nt) - nt * P, ROW), np.float32)
    pads[:, C_ID] = np.arange(nt * P, out_rows(nt))
    return pads


def laid_out(inputs):
    a = {k: np.asarray(v) for k, v in inputs.items()}

    def transposed(t):
        return t.transpose(0, 2, 1).reshape(-1, DT, P, S).transpose(0, 2, 1, 3)

    def by_dim(w):
        return w.reshape(-1, DT, HT, HD).transpose(0, 1, 3, 2).reshape(w.shape)

    p = "L0_xattn_"
    nt = a["x"].shape[0] * TT
    return {k: np.ascontiguousarray(v) for k, v in {
        "x": a["x"], "x_t": transposed(a["x"]), "ctx_t": transposed(a["ctx_1024"]),
        "wq": np.concatenate([by_dim(a[p + "Wq"].T), a["L0_ffn_router_w"].T], 1), "wk": by_dim(a[p + "Wk"].T), "wv": a[p + "Wv"].T, "wo": a[p + "Wo"].T,
        "bias": np.concatenate([by_dim(a[p + "bq"][None])[0], by_dim(a[p + "bk"][None])[0], a[p + "bv"], a[p + "bo"],
                                a["L0_ffn_router_b"]]),
        "bo_by_row": a[p + "bo"].reshape(DT, P).T,
        "wo_n": a[p + "Wo"], "rope": rope_table(),
        "expert_t": a["L0_ffn_expert_w"].transpose(2, 0, 1).reshape(DT, P, E, D).transpose(1, 0, 2, 3),
        "expert_b": a["L0_ffn_expert_b"], "route": route_table(nt), "pads": pad_rows(nt),
        "token_ids": np.arange(nt * P, dtype=np.float32).reshape(nt, P).T,
    }.items()}


def kernel(**inputs):
    import concourse.bacc as bacc
    from concourse.bass_utils import run_bass_kernel_spmd

    arrays = laid_out(inputs)
    nc = bacc.Bacc("TRN2", target_bir_lowering=False, num_devices=1)
    args = {k: nc.dram_tensor(f"in_{k}", v.shape, mybir.dt.from_np(v.dtype), kind="ExternalInput").ap() for k, v in arrays.items()}
    shape = arrays["x"].shape
    out = nc.dram_tensor("out", (out_rows(shape[0] * TT), D), F32, kind="ExternalOutput").ap()
    attention_moe(nc, **args, out=out, NB=arrays["x"].shape[0])
    r = run_bass_kernel_spmd(nc, [{f"in_{k}": v for k, v in arrays.items()}], core_ids=[0])
    return r.results[0]["out"][:shape[0] * S].reshape(shape)
```

```python
import concourse.bass as bass
from concourse import mybir
from contextlib import ExitStack
import numpy as np

F32 = mybir.dt.float32
BF16 = mybir.dt.bfloat16
I32 = mybir.dt.int32
ALU = mybir.AluOpType
ACT = mybir.ActivationFunctionType
AX = mybir.AxisListType

P = 128
D = 256
S = 256
H = 16
HD = D // H
DT = D // P
TT = S // P
HT = H // DT
NSLOT = 6
Q_PART = (0, 0, 0, 1, 1, 2)
K_PART = (0, 1, 2, 0, 1, 0)
MROW = NSLOT * HD
STACK = MROW + 3
VW = 32
SCALE = HD ** -0.5
EPS = 1e-5
E = 8
NBANK = 3
RING = 8
ROW = D + 4
C_RSTD, C_SHIFT, C_WEIGHT, C_ID = range(D, ROW)
ROUTE_OPS = 15
R_LESS, R_CHOSEN, R_COUNTED = 5, 8, 12
LOOP_FIRST = 4
ROPE_VECTOR = 2
USETS = 9
TBANK = 3

SMALL = (("t0", 2), ("q0", 3), ("q1", 3), ("m1", 0), ("n0", -1), ("n1", -1), ("k", 3),
         ("a", -1), ("t1", 2), ("o0", -1), ("m0", 1), ("o1", -1), ("c", -2), ("v", 1))
ORDER = [name for name, _ in SMALL]
BANK = dict(zip(ORDER, (0, 1, 2, 0, 1, 2, 0, 1, 2, 0, 2, 1, 0, 2)))
READ_BY = {"q0": ("q_moved", 2, 1), "q1": ("q_moved", 2, 2), "k": ("k_moved", 1, 1), "v": ("v_moved", 1, 1),
           "t0": ("rest_made", 2, 1), "t1": ("rest_made", 2, 2), "m0": ("max_moved", 2, 1),
           "m1": ("max_moved", 2, 2), "n0": ("heads_normed", 2, 1), "n1": ("heads_normed", 2, 2),
           "a": ("normed_moved", 1, 1), "o0": ("attn_added", 2, 1), "o1": ("attn_added", 2, 2),
           "c": ("routed", ROUTE_OPS, R_COUNTED)}


class Batch:

    def __init__(self, i, c, per=2):
        self.i, self.c, self.per = i, c, per

    def __add__(self, n):
        return Batch(self.i, self.c + n, self.per)

    @property
    def fixed(self):
        return isinstance(self.i, int)

    def times(self, a, b=0):
        k = a * self.c + b
        assert k >= 0 and (self.fixed or not b or k > 0)
        return k if self.fixed else self.i * (self.per * a) + k

    @property
    def par(self):
        return self.c % self.per

    def half(self, a, b=0):
        k = a * (self.c // self.per) + b
        assert k >= 0 and (self.fixed or not b or k > 0)
        return k if self.fixed else self.i * a + k

    def after(self, n):
        assert self.fixed or self.c >= n
        return self.c >= n

    def is_(self, n):
        return self.fixed and self.c == n

    def real(self, n):
        return not self.fixed or 0 <= self.c < n


def attention_moe(nc, x, x_t, ctx_t, wq, wk, wv, wo, wo_n, bias, bias_by_row, rope, expert_t, expert_b,
                  route, pads, token_ids, out, NB):
    NT = NB * TT
    NS = NT + E - 1
    DR = D + E
    REGION = (NT + 1) * P
    R_DESC, R_TILE, R_SLOT, R_BASE, R_ROW, R_TRI = np.cumsum([0, E, NT, NS, E, NS]).tolist()

    with ExitStack() as ctx:
        def sb(name, shape, dt=F32):
            return ctx.enter_context(nc.sbuf_tensor(name, shape, dt))

        def pb(name):
            return ctx.enter_context(nc.psum_tensor(name, [P, 512], F32))

        def sem(name):
            return ctx.enter_context(nc.semaphore(name))

        resid = sb("resid", [P, NB * TT, D])
        w_q, w_o = (sb(n, [P, DT, DR]) for n in ("w_q", "w_o"))
        w_k, w_v = (sb(n, [P, DT, D]) for n in ("w_k", "w_v"))
        biases = sb("biases", [P, 3 * D + E])
        b_q, b_k, b_o = (biases[:, D * n:D * (n + 1)] for n in range(3))
        b_r = biases[:, 3 * D:]
        cos_sin = sb("cos_sin", [P, 2, TT, D])
        avg = sb("avg", [P, P])
        ident = sb("ident", [P, P])
        ident_b = sb("ident_b", [P, P], BF16)
        powers = sb("powers", [P, TT])
        xt = [sb(f"xt{p}", [P, DT, S]) for p in range(2)]
        ct = [sb(f"ct{p}", [P, DT, S]) for p in range(2)]
        cv = [sb(f"cv{p}", [P, DT, S]) for p in range(2)]
        bn1 = sb("bn1", [P, TT, 6])
        mv1 = sb("mv1", [P, TT, 2])
        ve1 = sb("ve1", [P, 2, TT])
        rstd1 = sb("rstd1", [P, 2, TT])
        flat = sb("flat", [P, 2, TT, D])
        by_cos = sb("by_cos", [P, TT, D])
        by_sin = sb("by_sin", [P, TT, D])
        roped = [sb(f"roped{p}", [P, 2, TT, D]) for p in range(2)]
        part = [sb(f"part{t}", [P, 2, 3, S], BF16) for t in range(DT)]
        rest = sb("rest", [P, 2, S])
        stack = [sb(f"stack{p}", [P, H, 2, S], BF16) for p in range(2)]
        v_ext = [sb(f"v_ext{p}", [P, TT, H, VW]) for p in range(2)]
        nmax = sb("nmax", [P, DT, TT, HT])
        nrest = sb("nrest", [P, TT, HT])
        mpart = sb("mpart", [P, DT, TT, 3, HT], BF16)
        mrows = sb("mrows", [3 * HT, DT, S], BF16)
        prob = [sb(f"prob{n}", [P, TT, S]) for n in range(RING)]
        heads_t = sb("heads_t", [P, 4, S])
        rden = sb("rden", [P, TT, H])
        normed = sb("normed", [P, TT, D])
        normed_t = sb("normed_t", [P, DT, S])
        w_on = normed_t
        bo_col, bv_col = (normed[:, :, P * n:P * (n + 1)] for n in range(2))
        by_row = sb("by_row", [P, 2, DT])
        bv_o = sb("bv_o", [P, D])
        bo_r = sb("bo_r", [P, E])
        table = sb("table", [P, R_TRI + P])
        w_e = sb("w_e", [P, DT, E, D])
        b_e = sb("b_e", [P, E, D])
        ids = sb("ids", [P, NT])
        logit = sb("logit", [P, NT, E])
        row = [sb(f"row{p}", [P, TT, ROW]) for p in range(2)]
        bn2 = sb("bn2", [P, TT, 6])
        mv2 = sb("mv2", [P, TT, 2])
        ve2 = sb("ve2", [P, TT])
        logits = sb("logits", [P, TT, E])
        top = sb("top", [P, TT])
        less = sb("less", [P, TT, E])
        prob_e = sb("prob_e", [P, TT, E])
        mark = sb("mark", [P, TT, E])
        first = sb("first", [P, TT])
        chosen = sb("chosen", [P, TT, E], BF16)
        tri_b = sb("tri_b", [P, P], BF16)
        ones_b = sb("ones_b", [P, P], BF16)
        base = sb("base", [P, E])
        place = sb("place", [P, TT, E])
        slot_f = sb("slot_f", [P, TT])
        slot_i = [sb(f"slot_i{p}", [P, TT], I32) for p in range(2)]
        count = sb("count", [P, E])
        tiles_cmp = sb("tiles_cmp", [P, E, NS])
        tiles_hop = sb("tiles_hop", [P, E, NS])
        tiles_of = sb("tiles_of", [P, E])
        tiles_end = sb("tiles_end", [P, E])
        lead = sb("lead", [P, E + 1])
        hop = sb("hop", [P, E])
        expert_f = sb("expert_f", [P, NS])
        expert_i = sb("expert_i", [P, NS], I32)
        start_f = sb("start_f", [P, NS])
        start_i = sb("start_i", [P, NS], I32)
        sorted_x = [sb(f"sorted_x{n}", [P, ROW]) for n in range(USETS)]
        sorted_t = [sb(f"sorted_t{n}", [P, DT, P]) for n in range(TBANK)]
        index = [sb(f"index{n}", [P, 1], I32) for n in range(USETS)]
        spare = [b[:, n] for b in (by_cos, by_sin) for n in range(TT)]
        spare += [b[:, a, n] for b in (flat, *roped) for a in range(2) for n in range(TT)]
        sorted_n, spare = spare[:TBANK], spare[TBANK:]
        sorted_y, spare = spare[:TBANK], spare[TBANK:]
        done = spare[:USETS]

        ps_st = [pb(f"ps_st{n}") for n in range(2)]
        ps_sm = [pb(f"ps_sm{n}") for n in range(2)]
        ps_pv = pb("ps_pv")
        ps_x = [pb(f"ps_x{n}") for n in range(NBANK)]

        ps_turn = [ps_st[0], ps_st[1], ps_sm[0]]
        ps_made = [ps_sm[1], ps_pv, ps_x[2]]

        names = ["consts", "avg_made", "powers_made", "ident_made", "wq_in", "wk_in", "wv_in", "wo_in", "bias_in", "rope_in", "q_moved", "k_moved", "v_moved", "rest_made", "max_moved", "heads_normed",
                 "normed_moved", "attn_added", "q_made", "k_made", "v_made", "turned", "max_turned", "heads_turned",
                 "normed_turned", "projected", "scores_t", "scores", "exp_done", "max_done", "pv_done",
                 "pv_moved", "stats1", "ve1_done", "rstd1_done", "bo_added", "rope_cos", "rope_sin", "rope_done",
                 "part0_made", "part1_made", "part2_made", "max_split", "rden_done", "w_mean", "w_centred", "stats2", "ve2_done",
                 "rstd2_done", "router_made", "router_ready", "routed", "exps_done", "tri_made", "counted", "e_in",
                 "table_in", "planned", "padded", "e_normed", "e_turned", "e_moved", "e_made", "e_biased", "e_done", "waited"]
        s = {n: sem(n) for n in names}
        x_in = [sem(f"x_in{p}") for p in range(2)]
        xt_in = [sem(f"xt_in{p}") for p in range(2)]
        ct_in = [sem(f"ct_in{p}") for p in range(2)]
        cv_in = [sem(f"cv_in{p}") for p in range(2)]
        stack_in = [[sem(f"stack_in{p}_{t}") for t in range(DT)] for p in range(2)]
        mrow_in = [[sem(f"mrow_in{p}_{t}") for t in range(DT)] for p in range(2)]

        scattered = [sem(f"scattered{p}") for p in range(2)]
        sorted_in = [sem(f"sorted_in{n}") for n in range(USETS)]
        out_done = [sem(f"out_done{n}") for n in range(USETS)]
        by_expert = nc.dram_tensor("by_expert", [E * REGION + (E - 1) * P, ROW], F32).ap()

        def no_wait(eng):
            eng.sem_inc(s["waited"], 1)

        def steps(eng, step):
            first = LOOP_FIRST
            pairs = (NB - 5 + 1 - first) // 2
            assert 2 * pairs == E
            for b in range(-3, first):
                step(Batch(0, b))
            with eng.Fori(0, pairs) as i:
                step(Batch(i, first))
                step(Batch(i, first + 1))
            for b in range(first + 2 * pairs, NB + 2):
                step(Batch(0, b))

        def sorted_steps(eng, step, values=None, most=0, back=0):
            def some(i, first, n):
                got = {}
                if values is not None:
                    own = [c for c in range(first, first + n) if i is not None or 0 <= c - back < NS]
                    regs = [eng.alloc_register(f"value{c}") for c in own]
                    start = own[0] - back + (0 if i is None else i * USETS)
                    eng.load(regs, values[0:1, bass.ds(start, len(own))])
                    got = {c: eng.snap(r, donate=True, min_val=0, max_val=most) for c, r in zip(own, regs)}
                for c in range(first, first + n):
                    step(Batch(0 if i is None else i, c, USETS), got.get(c))
                if values is not None:
                    for r in regs:
                        eng.free_register(r)

            first = USETS + 1
            rounds = (NS - 1 - first) // USETS
            some(None, 0, first)
            with eng.Fori(0, rounds) as i:
                some(i, first, USETS)
            first += rounds * USETS
            some(None, first, NS + 1 - first)

        def wait_bank_read(eng, b, name):
            n, at = ORDER.index(name), b
            while True:
                n -= 1
                if n < 0:
                    n, at = len(ORDER) - 1, at + -1
                if BANK[ORDER[n]] != BANK[name]:
                    continue
                if isinstance(at.i, int) and at.c < -3:
                    return
                of = at + SMALL[n][1]
                if of.real(NB):
                    who, per, place = READ_BY[ORDER[n]]
                    eng.wait_ge(s[who], of.times(per, place))
                    return

        def rotate(eng, ve, b, qk):
            if not b.real(NB):
                return
            if b.is_(0) and qk == 0 or b.is_(ROPE_VECTOR) and qk == 0:
                eng.wait_ge(s["rope_in"], 16)
            if qk == 0:
                eng.wait_ge(s["q_moved"], b.times(2, 2))
            else:
                eng.wait_ge(s["k_moved"], b.times(1, 1))
            k = 2 * qk
            if qk or b.after(1):
                eng.wait_ge(s["rope_done"], b.times(2, qk))
            ve.tensor_tensor(by_cos[:], flat[:, qk], cos_sin[:, 0], ALU.mult).then_inc(s["rope_cos"], 1)
            src = flat[:, qk].rearrange("p n (t a c) -> p (n t) a c", t=DT, a=2)
            sin = cos_sin[:, 1].rearrange("p n (t a c) -> p (n t) a c", t=DT, a=2)
            dst = by_sin[:].rearrange("p n (t a c) -> p (n t) a c", t=DT, a=2)
            for a in range(2):
                ve.tensor_tensor(dst[:, :, a], src[:, :, 1 - a], sin[:, :, a], ALU.mult).then_inc(s["rope_sin"], 1)
            eng.wait_ge(s["rope_cos"], b.times(2, qk + 1))
            eng.wait_ge(s["rope_sin"], b.times(4, k + 2))
            if qk == 0 and b.after(2):
                eng.wait_ge(s["turned"], b.times(2, -2))
            ve.tensor_tensor(roped[b.par][:, qk], by_cos[:], by_sin[:], ALU.add).then_inc(s["rope_done"], 1)

        x_v = x.rearrange("b (t p) d -> p (b t) d", p=P)
        block = ctx.enter_context(nc.Block())

        @block.sync
        def _(sp):
            def load_t(b):
                if not b.real(NB):
                    return
                if b.after(2):
                    sp.wait_ge(s["q_made"], b.times(2, -2))
                    sp.wait_ge(s["k_made"], b.times(1, -1))
                sp.dma_start(xt[b.par][:], x_t[bass.ds(b.times(1), 1)].rearrange("b p t s -> p (b t) s")).then_inc(xt_in[b.par], 16)
                sp.dma_start(ct[b.par][:], ctx_t[bass.ds(b.times(1), 1)].rearrange("b p t s -> p (b t) s")).then_inc(ct_in[b.par], 16)

            def load_x(b):
                if not b.real(NB):
                    return
                tiles = bass.ds(b.times(TT), TT)
                sp.dma_start(resid[:, tiles], x_v[:, tiles]).then_inc(x_in[b.par], 16)

            def load_v(b):
                if not b.real(NB):
                    return
                if b.after(2):
                    sp.wait_ge(s["v_made"], b.times(1, -1))
                sp.dma_start(cv[b.par][:], ctx_t[bass.ds(b.times(1), 1)].rearrange("b p t s -> p (b t) s")).then_inc(cv_in[b.par], 16)

            def fill_stack(b, t):
                if not b.real(NB):
                    return
                sp.wait_ge(s["part2_made"], b.times(2, t + 1))
                no_wait(sp)
                if b.after(2):
                    sp.wait_ge(s["scores_t"], b.times(H, -2 * H + HT * (t + 1)))
                both = part[t][:].rearrange("p a n s -> p (a n) s")
                for slot in range(NSLOT):
                    first, second = Q_PART[slot], 3 + K_PART[slot]
                    sp.dma_start(stack[b.par][HD * slot:HD * (slot + 1), HT * t:HT * (t + 1)],
                                 both[:, first:second + 1:second - first]).then_inc(stack_in[b.par][t], 16)

            def fill_max(b, t):
                if not b.real(NB):
                    return
                sp.wait_ge(s["max_moved"], b.times(2, t + 1))
                sp.dma_start(stack[b.par][MROW:STACK, HT * t:HT * (t + 1), 0], mrows[:, t]).then_inc(mrow_in[b.par][t], 16)

            def rows_of(w):
                return w.rearrange("(t p) e -> p t e", p=P)

            sp.dma_start(w_q[:], rows_of(wq)).then_inc(s["wq_in"], 16)
            load_x(Batch(0, 0))
            load_t(Batch(0, 0))
            sp.dma_start(w_k[:], rows_of(wk)).then_inc(s["wk_in"], 16)
            sp.dma_start(biases[:], bias.partition_broadcast(P)).then_inc(s["bias_in"], 16)
            sp.dma_start(cos_sin[:], rope).then_inc(s["rope_in"], 16)
            sp.dma_start(w_on[:], rows_of(wo_n)).then_inc(s["wo_in"], 16)
            sp.dma_start(by_row[:], bias_by_row).then_inc(s["wo_in"], 16)
            sp.dma_start(w_o[:, :, 0:D], rows_of(wo)).then_inc(s["wo_in"], 16)
            load_t(Batch(0, 1))
            load_x(Batch(0, 1))
            sp.dma_start(w_v[:], rows_of(wv)).then_inc(s["wv_in"], 16)

            def step(b):
                if not b.is_(-3):
                    load_t(b + 4)
                    load_x(b + 4)
                load_v(b + 2)
                if b.is_(-2):
                    sp.dma_start(table[:], route).then_inc(s["table_in"], 16)
                    sp.dma_start(ids[:], token_ids).then_inc(s["table_in"], 16)
                fill_stack(b + 1, 1)
                fill_max(b, 1)
                fill_stack(b + 2, 0)
                fill_max(b + 1, 0)
                if b.is_(2):
                    sp.dma_start(by_expert[E * REGION:], pads[E * P:]).then_inc(s["padded"], 16)
                    sp.dma_start(by_expert[0:E * REGION].rearrange("(e r) c -> e r c", e=E)[:, 0:P],
                                 pads[0:E * P].rearrange("(e r) c -> e r c", e=E)).then_inc(s["padded"], 16)
                if not b.fixed:
                    e = bass.ds(b.i * 2 + (b.c - LOOP_FIRST), 1)
                    sp.dma_start(w_e[:, :, e].rearrange("p t e d -> p (t e) d"),
                                 expert_t[:, :, e].rearrange("p t e d -> p (t e) d")).then_inc(s["e_in"], 16)
                    sp.dma_start(b_e[:, e].rearrange("p e d -> p (e d)"),
                                 expert_b[e].rearrange("e d -> (e d)").partition_broadcast(P)).then_inc(s["e_in"], 16)

            steps(sp, step)

            sp.wait_ge(s["planned"], 1)
            for p in range(2):
                sp.wait_ge(scattered[p], 16 * TT * (NB // 2))
            sp.wait_ge(s["padded"], 16 * 2)

            def load_sorted(j, start):
                if not j.real(NS):
                    return
                if j.after(USETS):
                    sp.wait_ge(s["e_done"], j.times(1, 1 - USETS))
                    no_wait(sp)
                sp.dma_start(sorted_x[j.par][:], by_expert[bass.ds(start, P)]).then_inc(sorted_in[j.par], 16)

            sorted_steps(sp, load_sorted, start_i, E * REGION + (E - 2) * P)
            for n in range(USETS):
                sp.wait_ge(out_done[n], 16 * len(range(n, NS, USETS)))

        @block.tensor
        def _(pe):
            mm = nc.tensor.matmul

            pe.wait_ge(s["wq_in"], 16)
            pe.wait_ge(s["avg_made"], 1)
            for t in range(DT):
                last = mm(ps_pv[:, 0:DR], avg[:], w_q[:, t], start=t == 0, stop=t == DT - 1)
            last.then_inc(s["w_mean"], 1)

            def fold_router():
                pe.wait_ge(s["wo_in"], 16 * 3)
                for m in range(DT):
                    for t in range(DT):
                        last = mm(ps_st[0][:, E * m:E * (m + 1)], w_on[:, t, P * m:P * (m + 1)], w_q[:, t, D:],
                                  start=t == 0, stop=t == DT - 1)
                last.then_inc(s["router_made"], 1)

            def fold_bias():
                pe.wait_ge(s["router_ready"], 3)
                for t in range(DT):
                    mm(ps_st[1][:, 0:D], bv_col[:, t], w_o[:, t, 0:D], start=t == 0, stop=t == DT - 1)
                for t in range(DT):
                    mm(ps_st[1][:, D:DR], bv_col[:, t], w_o[:, t, D:], start=t == 0, stop=False)
                for t in range(DT):
                    last = mm(ps_st[1][:, D:DR], bo_col[:, t], w_q[:, t, D:], start=False, stop=t == DT - 1)
                last.then_inc(s["router_made"], 1)

            def project_q(b, n):
                if not b.real(NB):
                    return
                if n == 0:
                    if b.is_(0):
                        pe.wait_ge(s["w_centred"], DT)
                    pe.wait_ge(xt_in[b.par], b.half(16, 16))
                if b.is_(1) and n == 1:
                    pe.wait_ge(s["rest_made"], 2)
                else:
                    wait_bank_read(pe, b + -3, f"q{n}")
                for t in range(DT):
                    last = mm(ps_x[BANK[f"q{n}"]][:, 0:DR], xt[b.par][:, t, P * n:P * (n + 1)], w_q[:, t],
                              start=t == 0, stop=t == DT - 1)
                last.then_inc(s["q_made"], 1)

            def project_kv(b, step, name, n, src, w, arrived, made):
                if not b.real(NB):
                    return
                if n == 0:
                    if b.is_(0):
                        pe.wait_ge(s["wk_in" if name == "k" else "wv_in"], 16)
                    pe.wait_ge(arrived[b.par], b.half(16, 16))
                    wait_bank_read(pe, step, name)
                for t in range(DT):
                    last = mm(ps_x[BANK[name]][:, D * n:D * (n + 1)], src[b.par][:, t, P * n:P * (n + 1)], w[:, t],
                              start=t == 0, stop=t == DT - 1)
                if n == TT - 1:
                    last.then_inc(s[made], 1)

            def turn(b, t):
                if not b.real(NB):
                    return
                if b.is_(0) and t == 0:
                    pe.wait_ge(s["ident_made"], 4)
                pe.wait_ge(s["rope_done"], b.times(2, 2))
                if not b.is_(0):
                    wait_bank_read(pe, b + -2, f"t{t}")
                bank = ps_x[BANK[f"t{t}"]]
                for qk in range(2):
                    for n in range(TT):
                        last = nc.tensor.transpose(bank[:, S * qk + P * n:S * qk + P * (n + 1)],
                                                   roped[b.par][:, qk, n, P * t:P * (t + 1)], ident[:])
                last.then_inc(s["turned"], 1)

            def turn_max(b, step, t):
                if not b.real(NB):
                    return
                pe.wait_ge(s["max_split"], b.times(8, 4 * (t + 1)))
                wait_bank_read(pe, step, f"m{t}")
                bank = ps_x[BANK[f"m{t}"]][:].bitcast(BF16)
                for n in range(TT):
                    last = nc.tensor.transpose(bank[0:3 * HT, P * n:P * (n + 1)],
                                               mpart[:, t, n].rearrange("p a h -> p (a h)"), ident_b[:])
                last.then_inc(s["max_turned"], 1)

            def score_t(b, h):
                if not b.real(NB):
                    return
                if h == 0 and b.is_(0):
                    pe.wait_ge(s["consts"], 6)
                if h % HT == 0:
                    pe.wait_ge(mrow_in[b.par][h // HT], b.half(16, 16))
                if h >= 2 or b.after(1):
                    pe.wait_ge(s["exp_done"], b.times(H, h - 1))
                for n in range(TT):
                    last = mm(ps_st[h % 2][:, S * n:S * (n + 1)], stack[b.par][0:STACK, h, 1, P * n:P * (n + 1)],
                              stack[b.par][0:STACK, h, 0, :], start=True, stop=True)
                last.then_inc(s["scores_t"], 1)

            def score(b, h):
                if not b.real(NB):
                    return
                if h % HT == 0:
                    pe.wait_ge(stack_in[b.par][h // HT], b.half(16 * NSLOT, 16 * NSLOT))
                if h >= 2 or b.after(1):
                    pe.wait_ge(s["max_done"], b.times(H, h - 1))
                for n in range(TT):
                    last = mm(ps_sm[h % 2][:, S * n:S * (n + 1)], stack[b.par][0:MROW, h, 0, P * n:P * (n + 1)],
                              stack[b.par][0:MROW, h, 1, :], start=True, stop=True)
                last.then_inc(s["scores"], 1)

            def prob_v(b, g):
                if not b.real(NB):
                    return
                pe.wait_ge(s["exp_done"], b.times(H, 4 * g + 4))
                if g == 0:
                    pe.wait_ge(s["v_moved"], b.times(1, 1))
                if g % 2 == 0 and (g or b.after(1)):
                    pe.wait_ge(s["pv_moved"], b.times(2, g // 2))
                for n in range(TT):
                    for j in range(4):
                        h = 4 * g + j
                        last = mm(ps_pv[32 * j:32 * (j + 1), S * (g % 2):S * (g % 2 + 1)], v_ext[b.par][:, n, h, :],
                                  prob[h % RING][:, n, :], start=n == 0, stop=n == TT - 1)
                last.then_inc(s["pv_done"], 1)

            def turn_heads(b, n):
                if not b.real(NB):
                    return
                pe.wait_ge(s["pv_moved"], b.times(2, 2))
                wait_bank_read(pe, b + 1, f"n{n}")
                for g in range(4):
                    last = nc.tensor.transpose(ps_x[BANK[f"n{n}"]][:, P * g:P * (g + 1)], heads_t[:, g, P * n:P * (n + 1)], ident[:])
                last.then_inc(s["heads_turned"], 1)

            def turn_normed(b):
                if not b.real(NB):
                    return
                pe.wait_ge(s["heads_normed"], b.times(2, 2))
                wait_bank_read(pe, b + 1, "a")
                for t in range(DT):
                    for n in range(TT):
                        last = nc.tensor.transpose(ps_x[BANK["a"]][:, S * t + P * n:S * t + P * (n + 1)],
                                                   normed[:, n, P * t:P * (t + 1)], ident[:])
                last.then_inc(s["normed_turned"], 1)

            def project_out(b, n):
                if not b.real(NB):
                    return
                if n == 0:
                    pe.wait_ge(s["normed_moved"], b.times(1, 1))
                    if b.is_(0):
                        pe.wait_ge(s["router_ready"], 3)
                wait_bank_read(pe, b + 1, f"o{n}")
                for t in range(DT):
                    last = mm(ps_x[BANK[f"o{n}"]][:, 0:DR], normed_t[:, t, P * n:P * (n + 1)], w_o[:, t],
                              start=t == 0, stop=t == DT - 1)
                last.then_inc(s["projected"], 1)

            def count_chosen(b):
                if not b.real(NB):
                    return
                pe.wait_ge(s["routed"], b.times(ROUTE_OPS, R_CHOSEN))
                if b.is_(0):
                    pe.wait_ge(s["tri_made"], 2)
                wait_bank_read(pe, b + 2, "c")
                bank = ps_x[BANK["c"]]
                ch = [chosen[:, n] for n in range(TT)]
                mm(bank[:, 0:E], tri_b[:], ch[0], start=True, stop=True)
                mm(bank[:, E:2 * E], tri_b[:], ch[1], start=True, stop=False)
                mm(bank[:, E:2 * E], ones_b[:], ch[0], start=False, stop=True)
                mm(bank[:, 2 * E:3 * E], ones_b[:], ch[0], start=True, stop=False)
                mm(bank[:, 2 * E:3 * E], ones_b[:], ch[1], start=False, stop=True).then_inc(s["counted"], 1)

            def step(b):
                def k_of(n):
                    project_kv(b + 3, b, "k", n, ct, w_k, ct_in, "k_made")

                def v_of(n):
                    project_kv(b + 1, b, "v", n, cv, w_v, cv_in, "v_made")

                small = {
                    0: lambda: (turn(b + 2, 0), b.is_(-2) and turn(b + 2, 1)),
                    1: lambda: prob_v(b + -1, 3),
                    2: lambda: project_q(b + 3, 0),
                    3: lambda: (project_q(b + 3, 1), turn_max(b, b, 1)),
                    4: lambda: turn_heads(b + -1, 0),
                    5: lambda: turn_heads(b + -1, 1),
                    6: lambda: prob_v(b, 0),
                    7: lambda: k_of(0),
                    8: lambda: k_of(1),
                    9: lambda: (turn_normed(b + -1), b.is_(-2) or turn(b + 2, 1)),
                    10: lambda: prob_v(b, 1),
                    11: lambda: project_out(b + -1, 0),
                    12: lambda: (turn_max(b + 1, b, 0), project_out(b + -1, 1)),
                    13: lambda: (count_chosen(b + -2), prob_v(b, 2)),
                    14: lambda: v_of(0),
                    15: lambda: (v_of(1), b.is_(-2) and (fold_router(), fold_bias())),
                }
                for h in range(H):
                    score(b + 1, h)
                    score_t(b, h)
                    if h in small:
                        small[h]()

            steps(pe, step)

            pe.wait_ge(s["planned"], 2)
            pe.wait_ge(s["e_in"], 16 * 2 * E)

            def turn_sorted(j):
                if not j.real(NS):
                    return
                pe.wait_ge(s["e_normed"], j.times(1, 1))
                if j.after(TBANK):
                    pe.wait_ge(s["e_moved"], j.times(1, 1 - TBANK))
                n = j.par % TBANK
                for t in range(DT):
                    last = nc.tensor.transpose(ps_turn[n][:, P * t:P * (t + 1)], sorted_n[n][:, P * t:P * (t + 1)], ident[:])
                last.then_inc(s["e_turned"], 1)

            def expert(j, e):
                if not j.real(NS):
                    return
                pe.wait_ge(s["e_moved"], j.times(1, 1))
                if j.after(TBANK):
                    pe.wait_ge(s["e_biased"], j.times(1, 1 - TBANK))
                n = j.par % TBANK
                for t in range(DT):
                    last = mm(ps_made[n][:, 0:D], sorted_t[n][:, t], w_e[:, t, bass.ds(e, 1)].rearrange("p e d -> p (e d)"),
                              start=t == 0, stop=t == DT - 1)
                last.then_inc(s["e_made"], 1)

            sorted_steps(pe, lambda j, e: (turn_sorted(j), expert(j + -1, e)), expert_i, E - 1, back=1)

        @block.scalar
        def _(act):
            act.wait_ge(s["tri_made"], 1)
            for p in range(2):
                nc.scalar.copy(stack[p][MROW:P, :, 1], ones_b[MROW:P, 0:1].unsqueeze(2).to_broadcast([P - MROW, H, S]))\
                    .then_inc(s["consts"], 1)

            def exp(b, h):
                if not b.real(NB):
                    return
                act.wait_ge(s["scores_t"], b.times(H, h + 1))
                g = h // 4
                if g >= 2 or b.after(1):
                    act.wait_ge(s["pv_done"], b.times(4, g - 1))
                nc.scalar.activation(prob[h % RING][:].rearrange("p n s -> p (n s)"), ps_st[h % 2][:], ACT.Exp,
                                     scale=SCALE).then_inc(s["exp_done"], 1)

            def move_max(b, t):
                if not b.real(NB):
                    return
                act.wait_ge(s["max_turned"], b.times(2, t + 1))
                if b.after(1):
                    act.wait_ge(mrow_in[(b + -1).par][t], (b + -1).half(16, 16))
                nc.scalar.copy(mrows[:, t], ps_x[BANK[f"m{t}"]][:].bitcast(BF16)[0:3 * HT, 0:S]).then_inc(s["max_moved"], 1)

            def move_heads(b, half):
                if not b.real(NB):
                    return
                act.wait_ge(s["pv_done"], b.times(4, 2 * half + 2))
                if b.after(1):
                    act.wait_ge(s["heads_turned"], b.times(2))
                nc.scalar.copy(heads_t[:, 2 * half:2 * half + 2].rearrange("p g s -> p (g s)"), ps_pv[:]).then_inc(s["pv_moved"], 1)

            def part0(b, t):
                if not b.real(NB):
                    return
                act.wait_ge(s["turned"], b.times(2, t + 1))
                if b.after(1):
                    o = b + -1
                    act.wait_ge(stack_in[o.par][t], o.half(16 * NSLOT, 16 * NSLOT))
                nc.scalar.copy(part[t][:, :, 0], ps_x[BANK[f"t{t}"]][:].rearrange("p (a s) -> p a s", a=2)).then_inc(s["part0_made"], 1)

            def part1(b, t):
                if not b.real(NB):
                    return
                act.wait_ge(s["rest_made"], b.times(2, t + 1))
                nc.scalar.copy(part[t][:, :, 1], rest[:]).then_inc(s["part1_made"], 1)

            def move_folded():
                act.wait_ge(s["wo_in"], 16 * 3)
                for n, col in enumerate((bo_col, bv_col)):
                    nc.scalar.copy(col, by_row[:, n].unsqueeze(2).to_broadcast([P, DT, P])).then_inc(s["router_ready"], 1)
                act.wait_ge(s["router_made"], 1)
                nc.scalar.copy(w_o[:, :, D:], ps_st[0][:, 0:E * DT].rearrange("p (t e) -> p t e", t=DT)).then_inc(s["router_ready"], 1)
                act.wait_ge(s["router_made"], 2)
                nc.scalar.copy(bo_r[:], ps_st[1][:, D:DR]).then_inc(s["router_ready"], 1)
                nc.scalar.copy(bv_o[:], ps_st[1][:, 0:D]).then_inc(s["router_ready"], 1)

            def move_v(b):
                if not b.real(NB):
                    return
                act.wait_ge(s["v_made"], b.times(1, 1))
                if b.after(2):
                    act.wait_ge(s["pv_done"], b.times(4, -4))
                nc.scalar.copy(v_ext[b.par][:, :, :, 0:HD], ps_x[BANK["v"]][:].rearrange("p (n h e) -> p n h e", n=TT, h=H))\
                    .then_inc(s["v_moved"], 1)

            def move_normed(b):
                if not b.real(NB):
                    return
                act.wait_ge(s["normed_turned"], b.times(1, 1))
                if b.after(1):
                    act.wait_ge(s["projected"], b.times(2))
                nc.scalar.copy(normed_t[:].rearrange("p t s -> p (t s)"), ps_x[BANK["a"]][:]).then_inc(s["normed_moved"], 1)

            def exp_logits(b):
                if not b.real(NB):
                    return
                act.wait_ge(s["routed"], b.times(ROUTE_OPS, R_LESS))
                nc.scalar.activation(prob_e[:], less[:], ACT.Exp).then_inc(s["exps_done"], 1)

            def step(b):
                other = {
                    0: lambda: (part0(b + 2, 0), b.is_(-2) and part0(b + 2, 1)),
                    1: lambda: move_v(b),
                    2: lambda: move_heads(b + -1, 1),
                    3: lambda: (part1(b + 2, 0), move_max(b, 1)),
                    8: lambda: exp_logits(b + -2),
                    9: lambda: move_normed(b + -1),
                    10: lambda: b.is_(-2) or part0(b + 2, 1),
                    11: lambda: move_heads(b, 0),
                    12: lambda: move_max(b + 1, 0),
                    13: lambda: part1(b + 2, 1),
                }
                if b.is_(-1):
                    move_folded()
                for h in range(H):
                    exp(b, h)
                    if h in other:
                        other[h]()

            steps(act, step)

            def normalise(j):
                if not j.real(NS):
                    return
                x_in = sorted_x[j.par]
                act.wait_ge(sorted_in[j.par], j.half(16, 16))
                if j.after(TBANK):
                    act.wait_ge(s["e_turned"], j.times(1, 1 - TBANK))
                nc.scalar.activation(sorted_n[j.par % TBANK], x_in[:, 0:D], ACT.Identity, bias=x_in[:, C_SHIFT:C_SHIFT + 1],
                                     scale=x_in[:, C_RSTD:C_RSTD + 1]).then_inc(s["e_normed"], 1)

            def move_turned(j):
                if not j.real(NS):
                    return
                act.wait_ge(s["e_turned"], j.times(1, 1))
                if j.after(TBANK):
                    act.wait_ge(s["e_made"], j.times(1, 1 - TBANK))
                n = j.par % TBANK
                nc.scalar.copy(sorted_t[n][:].rearrange("p t s -> p (t s)"), ps_turn[n][:, 0:D]).then_inc(s["e_moved"], 1)

            normalise(Batch(0, 0, USETS))
            sorted_steps(act, lambda j, _: (normalise(j + 1), move_turned(j)))

        @block.vector
        def _(dve):
            v = nc.vector
            v.memset(avg[:], 1.0 / D).then_inc(s["avg_made"], 1)
            v.memset(ones_b[:], 1.0).then_inc(s["tri_made"], 1)
            dve.wait_ge(s["w_mean"], 1)
            for t in range(DT):
                v.tensor_tensor(w_q[:, t], w_q[:, t], ps_pv[:, 0:DR], ALU.subtract).then_inc(s["w_centred"], 1)
            def early_rotate(b, qk):
                if b.fixed and b.c < ROPE_VECTOR:
                    rotate(dve, v, b, qk)

            def take_max(b, h):
                if not b.real(NB):
                    return
                dve.wait_ge(s["scores"], b.times(H, h + 1))
                if h % HT == 0 and b.after(1):
                    dve.wait_ge(s["max_split"], b.times(8, 4 * (h // HT + 1) - 8))
                v.tensor_reduce(nmax[:, h // HT, :, h % HT], ps_sm[h % 2][:].rearrange("p (n s) -> p n s", n=TT), AX.X,
                                ALU.max, negate=True).then_inc(s["max_done"], 1)

            def split_max(b, t, n):
                if not b.real(NB):
                    return
                if n == 0:
                    dve.wait_ge(s["max_done"], b.times(H, HT * (t + 1)))
                    if b.after(1):
                        dve.wait_ge(s["max_turned"], b.times(2, t - 1))
                    op = v.tensor_copy(mpart[:, t, :, 0], nmax[:, t])
                else:
                    dve.wait_ge(s["max_split"], b.times(8, 4 * t + n))
                    if n == 1:
                        op = v.tensor_tensor(nrest[:], nmax[:, t], mpart[:, t, :, 0], ALU.subtract)
                    elif n == 2:
                        op = v.tensor_copy(mpart[:, t, :, 1], nrest[:])
                    else:
                        op = v.tensor_tensor(mpart[:, t, :, 2], nrest[:], mpart[:, t, :, 1], ALU.subtract)
                op.then_inc(s["max_split"], 1)

            def stats1(b, n):
                if not b.real(NB):
                    return
                if n == 0:
                    dve.wait_ge(x_in[b.par], b.half(16, 16))
                    no_wait(dve)
                v.bn_stats(bn1[:, n], resid[:, bass.ds(b.times(TT, n), 1)].rearrange("p a d -> p (a d)")).then_inc(s["stats1"], 1)

            def variance1(b):
                if not b.real(NB):
                    return
                for n in range(TT):
                    dve.wait_ge(s["stats1"], b.times(4, n + 1))
                    no_wait(dve)
                    v.bn_aggr(mv1[:, n], bn1[:, n]).then_inc(s["stats1"], 1)

            def variance1_eps(b):
                if not b.real(NB):
                    return
                dve.wait_ge(s["stats1"], b.times(4, 4))
                if b.after(2):
                    dve.wait_ge(s["rstd1_done"], b.times(1, -1))
                v.tensor_scalar(ve1[:, b.par], mv1[:, :, 1], EPS, None, ALU.add).then_inc(s["ve1_done"], 1)

            def move_q(b, n):
                if not b.real(NB):
                    return
                dve.wait_ge(s["q_made"], b.times(2, n + 1))
                if n == 0:
                    dve.wait_ge(s["rstd1_done"], b.times(1, 1))
                    if b.is_(0):
                        dve.wait_ge(s["bias_in"], 16)
                    if b.after(1):
                        dve.wait_ge(s["rope_sin"], b.times(4, -2))
                v.scalar_tensor_tensor(flat[:, 0, n], ps_x[BANK[f"q{n}"]][:, 0:D], rstd1[:, b.par, n:n + 1], b_q,
                                       ALU.mult, ALU.add)
                lg = logit[:, bass.ds(b.times(TT, n), 1)].rearrange("p a e -> p (a e)")
                if b.is_(2) and n == 0:
                    dve.wait_ge(s["router_ready"], 4)
                if b.is_(0) or b.is_(1):
                    v.tensor_copy(lg, ps_x[BANK[f"q{n}"]][:, D:DR]).then_inc(s["q_moved"], 1)
                else:
                    v.tensor_tensor(lg, ps_x[BANK[f"q{n}"]][:, D:DR], bo_r[:], ALU.add).then_inc(s["q_moved"], 1)

            def move_k(b):
                if not b.real(NB):
                    return
                dve.wait_ge(s["k_made"], b.times(1, 1))
                if b.after(1):
                    dve.wait_ge(s["rope_sin"], b.times(4))
                v.tensor_tensor(flat[:, 1], ps_x[BANK["k"]][:].rearrange("p (n e) -> p n e", n=TT),
                                b_k.unsqueeze(1).to_broadcast([P, TT, D]), ALU.add).then_inc(s["k_moved"], 1)

            def rest_of(b, t):
                if not b.real(NB):
                    return
                dve.wait_ge(s["part0_made"], b.times(2, t + 1))
                if t or b.after(1):
                    dve.wait_ge(s["part2_made"], b.times(2, t))
                v.tensor_tensor(rest[:], ps_x[BANK[f"t{t}"]][:].rearrange("p (a s) -> p a s", a=2),
                                part[t][:, :, 0], ALU.subtract).then_inc(s["rest_made"], 1)

            def invert_sums(b, n):
                if not b.real(NB):
                    return
                dve.wait_ge(s["heads_turned"], b.times(2, n + 1))
                pv = ps_x[BANK[f"n{n}"]][:].rearrange("p (h e) -> p h e", h=H)
                v.reciprocal(rden[:, n], pv[:, :, HD]).then_inc(s["rden_done"], 1)

            def norm_heads(b, n):
                if not b.real(NB):
                    return
                if n == 0 and b.after(1):
                    dve.wait_ge(s["normed_turned"], b.times(1))
                dve.wait_ge(s["rden_done"], b.times(2, n + 1))
                pv = ps_x[BANK[f"n{n}"]][:].rearrange("p (h e) -> p h e", h=H)
                v.tensor_tensor(normed[:, n].rearrange("p (h e) -> p h e", h=H), pv[:, :, 0:HD],
                                rden[:, n].unsqueeze(2).to_broadcast([P, H, HD]), ALU.mult).then_inc(s["heads_normed"], 1)

            def add_attn(b, n):
                if not b.real(NB):
                    return
                dve.wait_ge(s["projected"], b.times(2, n + 1))
                if n == 0:
                    dve.wait_ge(s["bo_added"], b.times(1, 1))
                    if b.is_(0):
                        dve.wait_ge(s["router_ready"], 7)
                    dve.wait_ge(s["q_moved"], b.times(2, 2))
                    if b.after(2):
                        dve.wait_ge(scattered[b.par], b.half(16 * TT))
                tile = bass.ds(b.times(TT, n), 1)
                v.tensor_tensor(logits[:, n], ps_x[BANK[f"o{n}"]][:, D:DR], logit[:, tile].rearrange("p a e -> p (a e)"), ALU.add)
                v.tensor_tensor(row[b.par][:, n, 0:D], ps_x[BANK[f"o{n}"]][:, 0:D], resid[:, tile].rearrange("p a d -> p (a d)"),
                                ALU.add).then_inc(s["attn_added"], 1)

            def stats2(b, n):
                if not b.real(NB):
                    return
                dve.wait_ge(s["attn_added"], b.times(2, n + 1))
                v.bn_stats(bn2[:, n], row[b.par][:, n, 0:D]).then_inc(s["stats2"], 1)

            def variance2(b):
                if not b.real(NB):
                    return
                for n in range(TT):
                    dve.wait_ge(s["stats2"], b.times(4, n + 1))
                    no_wait(dve)
                    v.bn_aggr(mv2[:, n], bn2[:, n]).then_inc(s["stats2"], 1)

            def variance2_eps(b):
                if not b.real(NB):
                    return
                dve.wait_ge(s["stats2"], b.times(4, 4))
                v.tensor_scalar(ve2[:], mv2[:, :, 1], EPS, None, ALU.add).then_inc(s["ve2_done"], 1)

            def per_tile(a):
                return a.unsqueeze(2).to_broadcast([P, TT, E])

            def each_tile(a):
                return a.unsqueeze(1).to_broadcast([P, TT, E])

            def route(b, n):
                if not b.real(NB):
                    return
                r = row[b.par]
                psum = ps_x[BANK["c"]]
                if n:
                    dve.wait_ge(s["routed"], b.times(ROUTE_OPS, n))
                if n == 0:
                    dve.wait_ge(s["rstd2_done"], b.times(1, 1))
                    op = v.tensor_tensor(logits[:], logits[:], per_tile(r[:, :, C_RSTD]), ALU.mult)
                elif n == 1:
                    op = v.scalar_tensor_tensor(r[:, :, C_SHIFT], mv2[:, :, 0], -1.0, r[:, :, C_RSTD], ALU.mult, ALU.mult)
                elif n == 2:
                    op = v.tensor_tensor(logits[:], logits[:], each_tile(b_r), ALU.add)
                elif n == 3:
                    op = v.tensor_reduce(top[:], logits[:], AX.X, ALU.max)
                elif n == 4:
                    op = v.tensor_tensor(less[:], logits[:], per_tile(top[:]), ALU.subtract)
                elif n == 5:
                    op = v.scalar_tensor_tensor(mark[:], less[:], 0.0, each_tile(table[:, R_DESC:R_DESC + E]),
                                                ALU.is_equal, ALU.mult)
                elif n == 6:
                    op = v.tensor_reduce(first[:], mark[:], AX.X, ALU.max)
                elif n == 7:
                    op = v.tensor_tensor(chosen[:], mark[:], per_tile(first[:]), ALU.is_equal)
                elif n == 8:
                    dve.wait_ge(s["exps_done"], b.times(1, 1))
                    op = v.tensor_reduce(top[:], prob_e[:], AX.X, ALU.add)
                elif n == 9:
                    op = v.reciprocal(r[:, :, C_WEIGHT], top[:])
                elif n == 10:
                    dve.wait_ge(s["counted"], b.times(1, 1))
                    op = v.tensor_tensor(place[:], psum[:, 0:TT * E].rearrange("p (n e) -> p n e", n=TT), each_tile(base[:]), ALU.add)
                elif n == 11:
                    op = v.tensor_tensor(base[:], psum[:, TT * E:(TT + 1) * E], base[:], ALU.add)
                elif n == 12:
                    op = v.tensor_tensor(place[:], place[:], chosen[:], ALU.mult)
                elif n == 13:
                    op = v.tensor_reduce(slot_f[:], place[:], AX.X, ALU.add)
                else:
                    op = v.tensor_copy(slot_i[b.par][:], slot_f[:])
                op.then_inc(s["routed"], 1)

            def number(b):
                if not b.real(NB):
                    return
                v.tensor_copy(row[b.par][:, :, C_ID], ids[:, bass.ds(b.times(TT), TT)])

            def step(b):
                if b.is_(-3):
                    for n in range(TT):
                        stats1(Batch(0, 0), n)
                    variance1(Batch(0, 0))
                    variance1_eps(Batch(0, 0))
                if b.is_(-1):
                    dve.wait_ge(s["table_in"], 16 * 2)
                    v.tensor_copy(tri_b[:], table[:, R_TRI:R_TRI + P]).then_inc(s["tri_made"], 1)
                    v.tensor_copy(base[:], table[:, R_BASE:R_BASE + E]).then_inc(s["tri_made"], 1)
                other = {
                    0: lambda: split_max(b, 1, 1),
                    1: lambda: split_max(b, 1, 2),
                    2: lambda: (split_max(b, 1, 3), rest_of(b + 2, 0), route(b + -2, 0)),
                    3: lambda: (move_q(b + 3, 0), b.is_(-2) and rest_of(b + 2, 1), route(b + -2, 1), route(b + -2, 2)),
                    4: lambda: (move_q(b + 3, 1), early_rotate(b + 3, 0), route(b + -2, 3)),
                    5: lambda: (invert_sums(b + -1, 0), route(b + -2, 4)),
                    6: lambda: (norm_heads(b + -1, 0), invert_sums(b + -1, 1), route(b + -2, 5)),
                    7: lambda: (norm_heads(b + -1, 1), route(b + -2, 6)),
                    8: lambda: (stats1(b + 4, 0), split_max(b + 1, 0, 0), route(b + -2, 7)),
                    9: lambda: (split_max(b + 1, 0, 1), move_k(b + 3), early_rotate(b + 3, 1),
                                split_max(b + 1, 0, 2)),
                    10: lambda: (split_max(b + 1, 0, 3), stats1(b + 4, 1), route(b + -2, 8)),
                    11: lambda: (b.is_(-2) or rest_of(b + 2, 1), route(b + -2, 9), variance1(b + 4)),
                    12: lambda: (add_attn(b + -1, 0), variance1_eps(b + 4)),
                    13: lambda: (add_attn(b + -1, 1), number(b + -1)),
                    14: lambda: (route(b + -2, 10), stats2(b + -1, 0), route(b + -2, 11), stats2(b + -1, 1)),
                    15: lambda: (route(b + -2, 12), variance2(b + -1), route(b + -2, 13), split_max(b + 1, 1, 0),
                                 variance2_eps(b + -1), route(b + -2, 14)),
                }
                urgent = (2, 3, 4, 11)
                for h in range(H):
                    if h in urgent:
                        other[h]()
                    take_max(b + 1, h)
                    if h in other and h not in urgent:
                        other[h]()

            steps(dve, step)

            made = [ROUTE_OPS * NB]

            def then(op):
                made[0] += 1
                op.then_inc(s["routed"], 1)
                dve.wait_ge(s["routed"], made[0])

            def per_expert(a, n):
                return a.unsqueeze(2).to_broadcast([P, E, n])

            def each_expert(lo, n):
                return table[:, lo:lo + n].unsqueeze(1).to_broadcast([P, E, n])

            then(v.tensor_tensor(count[:], base[:], table[:, R_BASE:R_BASE + E], ALU.subtract))
            then(v.tensor_tensor(tiles_cmp[:, :, 0:NT], per_expert(count[:], NT), each_expert(R_TILE, NT), ALU.is_gt))
            then(v.tensor_reduce(tiles_of[:], tiles_cmp[:, :, 0:NT], AX.X, ALU.add))
            then(v.tensor_tensor_scan(tiles_end[:], tiles_of[:], tiles_of[:], 0.0, ALU.add, ALU.bypass))
            then(v.scalar_tensor_tensor(lead[:, 0:E], tiles_end[:], -float(P), base[:], ALU.mult, ALU.add))
            then(v.tensor_scalar(lead[:, E:E + 1], tiles_end[:, E - 1:E], -float(P), float(E * REGION), ALU.mult, ALU.add))
            then(v.tensor_tensor(hop[:], lead[:, 1:E + 1], lead[:, 0:E], ALU.subtract))
            then(v.tensor_tensor(tiles_cmp[:], per_expert(tiles_end[:], NS), each_expert(R_SLOT, NS), ALU.is_le))
            then(v.tensor_tensor(tiles_hop[:], tiles_cmp[:], per_expert(hop[:], NS), ALU.mult))
            then(v.tensor_reduce(start_f[:], tiles_hop[:].rearrange("p e n -> p n e"), AX.X, ALU.add))
            v.scalar_tensor_tensor(start_i[:], start_f[:], lead[:, 0:1], table[:, R_ROW:R_ROW + NS],
                                   ALU.add, ALU.add).then_inc(s["planned"], 1)
            then(v.tensor_reduce(expert_f[:], tiles_cmp[:].rearrange("p e n -> p n e"), AX.X, ALU.add))
            v.tensor_scalar(expert_i[:], expert_f[:], float(E - 1), None, ALU.min).then_inc(s["planned"], 1)
            dve.wait_ge(s["planned"], 2)

            def add_bias(j, e):
                if not j.real(NS):
                    return
                n = j.par % TBANK
                dve.wait_ge(s["e_made"], j.times(1, 1))
                if j.after(TBANK):
                    dve.wait_ge(s["e_done"], j.times(1, 1 - TBANK))
                v.tensor_tensor(sorted_y[n], ps_made[n][:, 0:D], b_e[:, bass.ds(e, 1)].rearrange("p e d -> p (e d)"),
                                ALU.add).then_inc(s["e_biased"], 1)

            def finish(j):
                if not j.real(NS):
                    return
                x_in = sorted_x[j.par]
                dve.wait_ge(s["e_biased"], j.times(1, 1))
                if j.after(USETS):
                    dve.wait_ge(out_done[j.par], j.half(16))
                v.tensor_copy(index[j.par][:], x_in[:, C_ID:C_ID + 1])
                v.scalar_tensor_tensor(done[j.par], sorted_y[j.par % TBANK], x_in[:, C_WEIGHT:C_WEIGHT + 1], x_in[:, 0:D],
                                       ALU.mult, ALU.add).then_inc(s["e_done"], 1)

            sorted_steps(dve, lambda j, e: (add_bias(j, e), finish(j + -1)), expert_i, E - 1)

        @block.gpsimd
        def _(pool):
            g = nc.gpsimd
            g.memset(powers[:], -0.5).then_inc(s["powers_made"], 1)
            for m in (ident, ident_b):
                g.memset(m[:], 0.0).then_inc(s["ident_made"], 1)
            pool.wait_ge(s["ident_made"], 2)
            for m in (ident, ident_b):
                g.affine_select(out=m[:], in_=m[:], compare_op=ALU.not_equal, fill=1.0, base=0,
                                pattern=[[-1, P]], channel_multiplier=1).then_inc(s["ident_made"], 1)
            for p in range(2):
                g.memset(v_ext[p][:, :, :, HD:HD + 1], 1.0).then_inc(s["consts"], 1)
                g.memset(v_ext[p][:, :, :, HD + 1:], 0.0).then_inc(s["consts"], 1)

            def rstd1_of(b):
                if not b.real(NB):
                    return
                pool.wait_ge(s["ve1_done"], b.times(1, 1))
                if b.after(2):
                    pool.wait_ge(s["q_moved"], b.times(2, -2))
                g.tensor_tensor(rstd1[:, b.par], ve1[:, b.par], powers[:], ALU.pow).then_inc(s["rstd1_done"], 1)

            def rstd2_of(b):
                if not b.real(NB):
                    return
                pool.wait_ge(s["ve2_done"], b.times(1, 1))
                g.tensor_tensor(row[b.par][:, :, C_RSTD], ve2[:], powers[:], ALU.pow).then_inc(s["rstd2_done"], 1)

            def scatter(b):
                if not b.real(NB):
                    return
                pool.wait_ge(s["routed"], b.times(ROUTE_OPS, ROUTE_OPS))
                no_wait(pool)
                for n in range(TT):
                    g.indirect_dma_start(out=by_expert, out_offset=bass.IndirectOffsetOnAxis(ap=slot_i[b.par][:, n:n + 1], axis=0),
                                         in_=row[b.par][:, n], in_offset=None).then_inc(scattered[b.par], 16)

            def add_bias_sums():
                pool.wait_ge(s["router_ready"], 5)
                g.tensor_tensor(b_o, b_o, bv_o[:], ALU.add).then_inc(s["router_ready"], 1)
                pool.wait_ge(s["q_moved"], 4)
                early = logit[:, 0:2 * TT]
                g.tensor_tensor(early, early, bo_r[:].unsqueeze(1).to_broadcast([P, 2 * TT, E]), ALU.add).then_inc(s["router_ready"], 1)

            def add_bo(b):
                if not b.real(NB):
                    return
                if b.is_(0):
                    pool.wait_ge(s["router_ready"], 6)
                r = resid[:, bass.ds(b.times(TT), TT)]
                g.tensor_tensor(r, r, b_o.unsqueeze(1).to_broadcast([P, TT, D]), ALU.add).then_inc(s["bo_added"], 1)

            def part2(b, t):
                if not b.real(NB):
                    return
                pool.wait_ge(s["part1_made"], b.times(2, t + 1))
                g.tensor_tensor(part[t][:, :, 2], rest[:], part[t][:, :, 1], ALU.subtract).then_inc(s["part2_made"], 1)

            pool.wait_ge(s["powers_made"], 1)

            def step(b):
                if b.is_(-3):
                    rstd1_of(Batch(0, 0))
                part2(b + 2, 0)
                if b.is_(-2):
                    part2(b + 2, 1)
                if b.after(ROPE_VECTOR - 3):
                    rotate(pool, g, b + 3, 0)
                    rotate(pool, g, b + 3, 1)
                if not b.is_(-2):
                    part2(b + 2, 1)
                rstd1_of(b + 4)
                if b.is_(-1):
                    add_bias_sums()
                    add_bo(Batch(0, 0))
                if b.after(-1):
                    add_bo(b + 2)
                rstd2_of(b + -1)
                scatter(b + -2)

            steps(pool, step)

            def store_sorted(j, _):
                if not j.real(NS):
                    return
                pool.wait_ge(s["e_done"], j.times(1, 1))
                no_wait(pool)
                g.indirect_dma_start(out=out, out_offset=bass.IndirectOffsetOnAxis(ap=index[j.par][:], axis=0),
                                     in_=done[j.par], in_offset=None).then_inc(out_done[j.par], 16)

            sorted_steps(pool, store_sorted)


def rope_table():
    freq = (1.0 / np.float32(10000.0) ** (np.arange(0, HD, 2, dtype=np.float32) / np.float32(HD))).astype(np.float32)
    angle = np.arange(S, dtype=np.float32)[:, None] * freq[None]
    angle = np.concatenate([angle, angle], -1)
    cos, sin = np.cos(angle), np.sin(angle)
    sin[:, :HD // 2] *= -1
    t = np.stack([cos, sin]).astype(np.float32)
    t = np.broadcast_to(t[:, :, None, :, None], (2, S, DT, HD, HT)).reshape(2, TT, P, D)
    return np.ascontiguousarray(t.transpose(2, 0, 1, 3))


def route_table(nt):
    ns = nt + E - 1
    row = np.concatenate([np.arange(E, 0, -1), P * np.arange(nt), np.arange(ns), (nt + 1) * P * np.arange(E) + P, P * np.arange(ns)])
    return np.concatenate([np.broadcast_to(row, (P, row.size)), np.triu(np.ones((P, P)), 1)], 1).astype(np.float32)


def out_rows(nt):
    return (nt + 2 * E - 1) * P


def pad_rows(nt):
    pads = np.zeros((out_rows(nt) - nt * P, ROW), np.float32)
    pads[:, C_ID] = np.arange(nt * P, out_rows(nt))
    return pads


def laid_out(inputs):
    a = {k: np.asarray(v) for k, v in inputs.items()}

    def transposed(t):
        return t.transpose(0, 2, 1).reshape(-1, DT, P, S).transpose(0, 2, 1, 3)

    def by_dim(w):
        return w.reshape(-1, DT, HT, HD).transpose(0, 1, 3, 2).reshape(w.shape)

    p = "L0_xattn_"
    nt = a["x"].shape[0] * TT
    return {k: np.ascontiguousarray(v) for k, v in {
        "x": a["x"], "x_t": transposed(a["x"]), "ctx_t": transposed(a["ctx_1024"]),
        "wq": np.concatenate([by_dim(a[p + "Wq"].T), a["L0_ffn_router_w"].T], 1), "wk": by_dim(a[p + "Wk"].T), "wv": a[p + "Wv"].T, "wo": a[p + "Wo"].T,
        "bias": np.concatenate([by_dim(a[p + "bq"][None])[0], by_dim(a[p + "bk"][None])[0], a[p + "bo"],
                                a["L0_ffn_router_b"]]),
        "bias_by_row": np.stack([a[p + "bo"], a[p + "bv"]]).reshape(2, DT, P).transpose(2, 0, 1),
        "wo_n": a[p + "Wo"], "rope": rope_table(),
        "expert_t": a["L0_ffn_expert_w"].transpose(2, 0, 1).reshape(DT, P, E, D).transpose(1, 0, 2, 3),
        "expert_b": a["L0_ffn_expert_b"], "route": route_table(nt), "pads": pad_rows(nt),
        "token_ids": np.arange(nt * P, dtype=np.float32).reshape(nt, P).T,
    }.items()}


def kernel(**inputs):
    import concourse.bacc as bacc
    from concourse.bass_utils import run_bass_kernel_spmd

    arrays = laid_out(inputs)
    nc = bacc.Bacc("TRN2", target_bir_lowering=False, num_devices=1)
    args = {k: nc.dram_tensor(f"in_{k}", v.shape, mybir.dt.from_np(v.dtype), kind="ExternalInput").ap() for k, v in arrays.items()}
    shape = arrays["x"].shape
    out = nc.dram_tensor("out", (out_rows(shape[0] * TT), D), F32, kind="ExternalOutput").ap()
    attention_moe(nc, **args, out=out, NB=arrays["x"].shape[0])
    r = run_bass_kernel_spmd(nc, [{f"in_{k}": v for k, v in arrays.items()}], core_ids=[0])
    return r.results[0]["out"][:shape[0] * S].reshape(shape)
```
